# Optimizing a Trainium2 kernel written in Bass

```python
import numpy as np
import jax
import jax.numpy as jnp

def _softmax(x, axis=-1):
    return jax.nn.softmax(x, axis=axis)

def _gelu(x):
    return jax.nn.gelu(x, approximate=True)

def _silu(x):
    return jax.nn.silu(x)

def _sigmoid(x):
    return jax.nn.sigmoid(x)

def _layernorm(x, axis=-1, eps=1e-05):
    m = jnp.mean(x, axis=axis, keepdims=True)
    v = jnp.var(x, axis=axis, keepdims=True)
    return (x - m) / jnp.sqrt(v + eps)

def _scatter_add(tgt, idx, src, axis=0):
    return tgt.at[idx].add(src)

def _segment_sum(src, seg, n):
    return jax.ops.segment_sum(src, seg, n)
kernel_name = 'mk_decoder_preln_d4_seqx_r8_a0a6e4'

def setup_inputs(seed: int=0):
    np.random.seed(seed)
    _w = jnp.asarray

    def _rec_inputs():
        import jax
        import jax.numpy as jnp
        _rk = jax.random.key(seed)
        x = -0.0002928 + 1 * jax.random.normal(jax.random.fold_in(_rk, 1), (16, 128, 128), jnp.float32)
        _lenS = 128 - jax.random.randint(jax.random.fold_in(_rk, 7), (16,), 0, max(1, 128 // 4) + 1, jnp.int32)
        _lenS2 = 128 - jax.random.randint(jax.random.fold_in(_rk, 8), (16,), 0, max(1, 128 // 4) + 1, jnp.int32)
        _ctx_1024P = jax.random.normal(jax.random.fold_in(_rk, 11), (16, 16, 128), jnp.float32)
        _ctx_1024c = jax.random.dirichlet(jax.random.fold_in(_rk, 511), 0.3 * jnp.ones((16,), jnp.float32), (16, 128))
        _ctx_1024t = jnp.einsum('bsk,bkd->bsd', _ctx_1024c, _ctx_1024P)
        _ctx_1024t = _ctx_1024t * jax.lax.rsqrt(jnp.mean(jnp.square(_ctx_1024t)) + 1e-12) * 0.953939
        ctx_1024 = -1.39393e-06 + 0.999914 * (_ctx_1024t + 0.3 * jax.random.normal(jax.random.fold_in(_rk, 611), (16, 128, 128), jnp.float32))
        fside_SxS2_0 = 0.000376506 + 0.999991 * jax.random.normal(jax.random.fold_in(_rk, 12), (128, 128), jnp.float32)
        return (x, ctx_1024, fside_SxS2_0)
    x, ctx_1024, fside_SxS2_0 = _rec_inputs()

    def _L0_attn_setup():
        import jax, jax.numpy as jnp
        import numpy as np
        import math
        N_HEAD = 16
        HEAD_QKV = 128
        WM_DECAY_LENGTH = 256
        WM_DECAY_RATE = 1.0
        WM_ECHOIC = 16

        def decay_weight_matrix(n):
            dl = WM_DECAY_LENGTH - WM_ECHOIC + 1
            nums = jnp.linspace(0.0, 1.0, dl)
            decay_values = 1.0 - jnp.power(nums, 1.0 / (np.e * WM_DECAY_RATE))
            decay_values = jnp.concatenate([jnp.ones(WM_ECHOIC - 1), decay_values])
            decay_values = decay_values[:n]
            idx = jnp.arange(n)[:, None] - jnp.arange(n)[None, :]
            mat = decay_values[jnp.clip(idx, 0, n - 1)]
            return jnp.tril(mat).astype(jnp.float32)
        key = jax.random.key(seed)
        k1, k2, k3 = jax.random.split(key, 3)
        B, T, C = (2, 256, 128)
        x = jax.random.normal(k1, (B, T, C), dtype=jnp.float32)
        W_attn = jax.random.normal(k2, (C, 3 * HEAD_QKV), dtype=jnp.float32) * (1.0 / math.sqrt(C))
        W_proj = jax.random.normal(k3, (HEAD_QKV, C), dtype=jnp.float32) * (1.0 / math.sqrt(HEAD_QKV))
        return {'x': x, 'W_attn': W_attn, 'W_proj': W_proj}
    _L0_attn_all = _L0_attn_setup()
    _L0_attn_in = {k: v for k, v in _L0_attn_all.items() if k in ('W_attn', 'W_proj')}
    del _L0_attn_all

    def _L0_xattn_setup():
        import jax, jax.numpy as jnp
        import numpy as np
        B, S, DIM, NH = (2, 256, 128, 8)
        DH = DIM // NH
        GATE_SOFT_CAP = 15.0
        BACKEND_EPS = 5e-05
        NORM_EPS = 1e-06

        def _mlstm_parallel(q, k, v, i_pre, f_pre):
            log_fg = jax.nn.log_sigmoid(f_pre)
            lf_cs = jnp.cumsum(log_fg, axis=-1)
            lf = jnp.concatenate([jnp.zeros_like(lf_cs[..., :1]), lf_cs], axis=-1)
            log_d = lf[..., 1:, None] - lf[..., None, 1:] + i_pre[..., None, :]
            t_idx = jnp.arange(q.shape[2])
            mask = t_idx[:, None] >= t_idx[None, :]
            log_d = jnp.where(mask, log_d, -jnp.inf)
            m = jnp.max(log_d, axis=-1, keepdims=True)
            d_mat = jnp.exp(log_d - m)
            scores = jnp.einsum('bhtd,bhsd->bhts', q, k) * (1.0 / np.sqrt(DH))
            s_mat = scores * d_mat
            denom = jnp.maximum(jnp.abs(jnp.sum(s_mat, axis=-1, keepdims=True)), jnp.exp(-m)) + BACKEND_EPS
            return jnp.einsum('bhts,bhsd->bhtd', s_mat, v) / denom
        key = jax.random.key(seed)
        kq, kk, kv, kw = jax.random.split(key, 4)
        q = jax.random.normal(kq, (B, S, DIM), dtype=jnp.float32)
        k = jax.random.normal(kk, (B, S, DIM), dtype=jnp.float32)
        v = jax.random.normal(kv, (B, S, DIM), dtype=jnp.float32)
        ifgate_w = 0.02 * jax.random.normal(kw, (2 * NH, 3 * DIM), dtype=jnp.float32)
        ifgate_b = jnp.concatenate([jnp.full((NH,), -10.0, dtype=jnp.float32), jnp.linspace(3.0, 6.0, NH, dtype=jnp.float32)])
        outnorm_w = jnp.zeros((DIM,), dtype=jnp.float32)
        return {'q': q, 'k': k, 'v': v, 'ifgate_w': ifgate_w, 'ifgate_b': ifgate_b, 'outnorm_w': outnorm_w}
    _L0_xattn_all = _L0_xattn_setup()
    _L0_xattn_in = {k: v for k, v in _L0_xattn_all.items() if k in ('ifgate_w', 'ifgate_b', 'outnorm_w')}
    del _L0_xattn_all

    def _L0_ffn_setup():
        import jax, jax.numpy as jnp
        import numpy as np
        D_MODEL = 128
        N_EXPERTS = 8
        TOP_K = 2
        BOTTLENECK = 64
        B, S = (2, 512)
        ADAPTER_SCALE = 0.5

        def _moe_forward(x, w_gate, w_noise, Wd, bd, Wu, bu):
            b, s, d = x.shape
            xf = x.reshape(-1, d)
            T = xf.shape[0]
            clean_logits = xf @ w_gate
            logits = clean_logits
            k1 = min(TOP_K + 1, N_EXPERTS)
            top_logits, top_idx = jax.lax.top_k(logits, k1)
            top_k_logits = top_logits[:, :TOP_K]
            top_k_idx = top_idx[:, :TOP_K]
            top_k_gates = jax.nn.softmax(top_k_logits, axis=-1)
            rows = jnp.arange(T)[:, None]
            gates = jnp.zeros((T, N_EXPERTS), dtype=top_k_gates.dtype)
            gates = gates.at[rows, top_k_idx].set(top_k_gates)
            h = jax.nn.relu(jnp.einsum('td,edb->teb', xf, Wd) + bd[None, :, :])
            y = jnp.einsum('teb,ebd->ted', h, Wu) + bu[None, :, :]
            y = ADAPTER_SCALE * y
            out = jnp.einsum('te,ted->td', gates, y)
            return out.reshape(b, s, d)
        key = jax.random.key(seed)
        ks = jax.random.split(key, 8)
        sd = 0.02
        x = jax.random.normal(ks[0], (B, S, D_MODEL), dtype=jnp.float32)
        w_gate = jax.random.normal(ks[1], (D_MODEL, N_EXPERTS), dtype=jnp.float32) * sd
        w_noise = jax.random.normal(ks[2], (D_MODEL, N_EXPERTS), dtype=jnp.float32) * sd
        Wd = jax.random.normal(ks[3], (N_EXPERTS, D_MODEL, BOTTLENECK), dtype=jnp.float32) * sd
        bd = jnp.zeros((N_EXPERTS, BOTTLENECK), dtype=jnp.float32)
        Wu = jax.random.normal(ks[4], (N_EXPERTS, BOTTLENECK, D_MODEL), dtype=jnp.float32) * sd
        bu = jnp.zeros((N_EXPERTS, D_MODEL), dtype=jnp.float32)
        return {'x': x, 'w_gate': w_gate, 'w_noise': w_noise, 'Wd': Wd, 'bd': bd, 'Wu': Wu, 'bu': bu}
    _L0_ffn_all = _L0_ffn_setup()
    _L0_ffn_in = {k: v for k, v in _L0_ffn_all.items() if k in ('w_gate', 'w_noise', 'Wd', 'bd', 'Wu', 'bu')}
    del _L0_ffn_all

    def _L1_attn_setup():
        import jax, jax.numpy as jnp
        import numpy as np
        EMBED_DIM = 128
        NUM_HEADS = 16
        HEAD_DIM = EMBED_DIM // NUM_HEADS
        key = jax.random.key(seed)
        k1, k2, k3 = jax.random.split(key, 3)
        inputs = jax.random.normal(k1, (4, 256, EMBED_DIM), dtype=jnp.float32)
        rotation_params = jax.random.normal(k2, (NUM_HEADS, HEAD_DIM), dtype=jnp.float32)
        entangle_params = jax.random.normal(k3, (NUM_HEADS, HEAD_DIM), dtype=jnp.float32)
        return {'inputs': inputs, 'rotation_params': rotation_params, 'entangle_params': entangle_params}
    _L1_attn_all = _L1_attn_setup()
    _L1_attn_in = {k: v for k, v in _L1_attn_all.items() if k in ('rotation_params', 'entangle_params')}
    del _L1_attn_all

    def _L1_xattn_setup():
        import jax, jax.numpy as jnp
        import numpy as np
        DIM = 128
        CTX_DIM = 128
        HEADS = 16
        DIM_HEAD = 64
        INNER = HEADS * DIM_HEAD
        FF_INNER = 4 * DIM
        EPS = 1e-05

        def layer_norm(x, g, b):
            mu = jnp.mean(x, axis=-1, keepdims=True)
            var = jnp.var(x, axis=-1, keepdims=True)
            return (x - mu) * jax.lax.rsqrt(var + EPS) * g + b
        key = jax.random.key(seed)
        ks = jax.random.split(key, 9)
        b, n, j = (4, 256, 128)
        inp = {'x': jax.random.normal(ks[0], (b, n, DIM), dtype=jnp.float32), 'context': jax.random.normal(ks[1], (b, j, CTX_DIM), dtype=jnp.float32), 'ln_g': jnp.ones((DIM,), jnp.float32), 'ln_b': jnp.zeros((DIM,), jnp.float32), 'cln_g': jnp.ones((CTX_DIM,), jnp.float32), 'cln_b': jnp.zeros((CTX_DIM,), jnp.float32), 'Wq': jax.random.normal(ks[2], (DIM, INNER), dtype=jnp.float32) * DIM ** (-0.5), 'Wkv': jax.random.normal(ks[3], (CTX_DIM, 2 * DIM_HEAD), dtype=jnp.float32) * CTX_DIM ** (-0.5), 'Wo': jax.random.normal(ks[4], (INNER, DIM), dtype=jnp.float32) * INNER ** (-0.5), 'Wff1': jax.random.normal(ks[5], (DIM, 2 * FF_INNER), dtype=jnp.float32) * DIM ** (-0.5), 'Wff2': jax.random.normal(ks[6], (FF_INNER, DIM), dtype=jnp.float32) * FF_INNER ** (-0.5)}
        return inp
    _L1_xattn_all = _L1_xattn_setup()
    _L1_xattn_in = {k: v for k, v in _L1_xattn_all.items() if k in ('ln_g', 'ln_b', 'cln_g', 'cln_b', 'Wq', 'Wkv', 'Wo', 'Wff1', 'Wff2')}
    del _L1_xattn_all

    def _L1_ffn_setup():
        import jax, jax.numpy as jnp
        import numpy as np
        LORA_DIM = 16
        LORA_TOKEN_INDEX = 1
        B, S, D, H = (4, 256, 128, 512)
        key = jax.random.key(seed)
        ks = jax.random.split(key, 6)
        x = jax.random.normal(ks[0], (B, S, D), dtype=jnp.float32)
        W1 = jax.random.normal(ks[1], (H, D), dtype=jnp.float32) * 0.02
        b1 = jnp.zeros((H,), dtype=jnp.float32)
        W2 = jax.random.normal(ks[2], (D, H), dtype=jnp.float32) * 0.02
        b2 = jnp.zeros((D,), dtype=jnp.float32)
        scale = jnp.asarray(0.001, dtype=jnp.float32)
        return {'x': x, 'W1': W1, 'b1': b1, 'W2': W2, 'b2': b2, 'scale': scale}
    _L1_ffn_all = _L1_ffn_setup()
    _L1_ffn_in = {k: v for k, v in _L1_ffn_all.items() if k in ('W1', 'b1', 'W2', 'b2', 'scale')}
    del _L1_ffn_all

    def _L2_attn_setup():
        import jax, jax.numpy as jnp
        import numpy as np
        from jax import lax
        D_MODEL = 128
        D_INNER = 2 * D_MODEL
        D_STATE = 16
        D_CONV = 4
        DT_RANK = 64
        DT_MIN = 0.001
        DT_MAX = 0.1
        BATCH = 4
        SEQ = 256
        key = jax.random.key(seed)
        ks = jax.random.split(key, 8)
        s = lambda fan_in: 1.0 / np.sqrt(fan_in)
        x = jax.random.normal(ks[0], (BATCH, SEQ, D_MODEL), dtype=jnp.float32)
        W_in = jax.random.uniform(ks[1], (D_MODEL, 2 * D_INNER), jnp.float32, -s(D_MODEL), s(D_MODEL))
        conv_w = jax.random.uniform(ks[2], (D_INNER, 1, D_CONV), jnp.float32, -s(D_CONV), s(D_CONV))
        conv_b = jax.random.uniform(ks[3], (D_INNER,), jnp.float32, -s(D_CONV), s(D_CONV))
        W_x = jax.random.uniform(ks[4], (D_INNER, DT_RANK + 2 * D_STATE), jnp.float32, -s(D_INNER), s(D_INNER))
        W_dt = jax.random.uniform(ks[5], (DT_RANK, D_INNER), jnp.float32, -s(DT_RANK), s(DT_RANK))
        b_dt = jax.random.uniform(ks[6], (D_INNER,), jnp.float32, -s(DT_RANK), s(DT_RANK))
        A_log = jnp.log(jnp.broadcast_to(jnp.arange(1, D_STATE + 1, dtype=jnp.float32), (D_INNER, D_STATE)))
        D_param = jnp.ones((D_INNER,), dtype=jnp.float32)
        W_out = jax.random.uniform(ks[7], (D_INNER, D_MODEL), jnp.float32, -s(D_INNER), s(D_INNER))
        return {'x': x, 'W_in': W_in, 'conv_w': conv_w, 'conv_b': conv_b, 'W_x': W_x, 'W_dt': W_dt, 'b_dt': b_dt, 'A_log': A_log, 'D_param': D_param, 'W_out': W_out}
    _L2_attn_all = _L2_attn_setup()
    _L2_attn_in = {k: v for k, v in _L2_attn_all.items() if k in ('W_in', 'conv_w', 'conv_b', 'W_x', 'W_dt', 'b_dt', 'A_log', 'D_param', 'W_out')}
    del _L2_attn_all

    def _L2_xattn_setup():
        import jax, jax.numpy as jnp
        import numpy as np
        D_MODEL, D_HEAD, N_HEAD = (128, 64, 16)
        B, T1, T2 = (2, 256, 256)
        key = jax.random.key(seed)
        ks = jax.random.split(key, 8)
        s = 1.0 / np.sqrt(D_MODEL)
        return {'x': jax.random.normal(ks[0], (B, T1, D_MODEL), dtype=jnp.float32), 'context': jax.random.normal(ks[1], (B, T2, D_MODEL), dtype=jnp.float32), 'bias': jax.random.normal(ks[2], (T1, T2), dtype=jnp.float32), 'W_q': jax.random.normal(ks[3], (D_MODEL, N_HEAD * D_HEAD), dtype=jnp.float32) * s, 'W_k': jax.random.normal(ks[4], (D_MODEL, N_HEAD * D_HEAD), dtype=jnp.float32) * s, 'W_v': jax.random.normal(ks[5], (D_MODEL, N_HEAD * D_HEAD), dtype=jnp.float32) * s, 'W_out': jax.random.normal(ks[6], (N_HEAD * D_HEAD, D_MODEL), dtype=jnp.float32) * s, 'b_out': jnp.zeros((D_MODEL,), dtype=jnp.float32)}
    _L2_xattn_all = _L2_xattn_setup()
    _L2_xattn_in = {k: v for k, v in _L2_xattn_all.items() if k in ('W_q', 'W_k', 'W_v', 'W_out', 'b_out')}
    del _L2_xattn_all

    def _L2_ffn_setup():
        import jax, jax.numpy as jnp
        import numpy as np
        BLOCK = 16
        _GRID = jnp.array([0.0, 0.5, 1.0, 1.5, 2.0, 3.0, 4.0, 6.0], dtype=jnp.float32)
        _MID = jnp.array([0.25, 0.75, 1.25, 1.75, 2.5, 3.5, 5.0], dtype=jnp.float32)

        def fp4_quant_dequant(x):
            shape = x.shape
            xb = x.reshape(shape[:-1] + (shape[-1] // BLOCK, BLOCK))
            scale = jnp.max(jnp.abs(xb), axis=-1, keepdims=True) / 6.0
            scale = jnp.maximum(scale, jnp.float32(1e-12))
            xn = xb / scale
            idx = jnp.searchsorted(_MID, jnp.abs(xn))
            q = _GRID[idx] * jnp.sign(xn) * scale
            return q.reshape(shape)

        def fp4_linear(x, w):
            xq = fp4_quant_dequant(x)
            wq = fp4_quant_dequant(w)
            return jnp.einsum('bsk,nk->bsn', xq, wq)
        key = jax.random.key(seed)
        k1, k2, k3, k4 = jax.random.split(key, 4)
        H, I = (128, 352)
        x = jax.random.normal(k1, (4, 512, H), dtype=jnp.float32)
        w_gate = jax.random.normal(k2, (I, H), dtype=jnp.float32) * 0.02
        w_up = jax.random.normal(k3, (I, H), dtype=jnp.float32) * 0.02
        w_down = jax.random.normal(k4, (H, I), dtype=jnp.float32) * 0.02
        return {'x': x, 'w_gate': w_gate, 'w_up': w_up, 'w_down': w_down}
    _L2_ffn_all = _L2_ffn_setup()
    _L2_ffn_in = {k: v for k, v in _L2_ffn_all.items() if k in ('w_gate', 'w_up', 'w_down')}
    del _L2_ffn_all

    def _L3_attn_setup():
        import jax, jax.numpy as jnp
        import numpy as np
        HIDDEN, HEADS, HDIM = (128, 8, 64)
        B, S = (4, 1024)
        LN_EPS = 1e-06
        key = jax.random.key(seed)
        ks = jax.random.split(key, 12)
        inner = HEADS * HDIM
        sd = HIDDEN ** (-0.5)
        return {'x': jax.random.normal(ks[0], (B, S, HIDDEN), jnp.float32), 'Wq': jax.random.normal(ks[1], (HIDDEN, inner), jnp.float32) * sd, 'bq': jnp.zeros((inner,), jnp.float32), 'Wk': jax.random.normal(ks[2], (HIDDEN, inner), jnp.float32) * sd, 'bk': jnp.zeros((inner,), jnp.float32), 'Wv': jax.random.normal(ks[3], (HIDDEN, inner), jnp.float32) * sd, 'bv': jnp.zeros((inner,), jnp.float32), 'Wo': jax.random.normal(ks[4], (inner, HIDDEN), jnp.float32) * inner ** (-0.5), 'bo': jnp.zeros((HIDDEN,), jnp.float32), 'alpha': jnp.ones((HEADS, HDIM), jnp.float32), 'aug_param': jax.random.normal(ks[5], (1, HEADS, HDIM), jnp.float32), 'ln_scale': jnp.ones((HIDDEN,), jnp.float32), 'ln_bias': jnp.zeros((HIDDEN,), jnp.float32)}
    _L3_attn_all = _L3_attn_setup()
    _L3_attn_in = {k: v for k, v in _L3_attn_all.items() if k in ('Wq', 'bq', 'Wk', 'bk', 'Wv', 'bv', 'Wo', 'bo', 'alpha', 'aug_param', 'ln_scale', 'ln_bias')}
    del _L3_attn_all

    def _L3_xattn_setup():
        import jax, jax.numpy as jnp
        import numpy as np
        B_SZ, T_LEN, C_DIM = (4, 512, 128)

        def _wkv_scan(ek, v, ew):

            def step(carry, xt):
                A, Bd = carry
                ekt, vt = xt
                out = (A, Bd)
                A2 = ew * A + ekt * vt
                B2 = ew * Bd + ekt
                return ((A2, B2), out)
            init = (jnp.zeros_like(ek[:, 0]), jnp.zeros_like(ek[:, 0]))
            xs = (jnp.moveaxis(ek, 1, 0), jnp.moveaxis(v, 1, 0))
            _, (A, Bd) = jax.lax.scan(step, init, xs)
            return (jnp.moveaxis(A, 0, 1), jnp.moveaxis(Bd, 0, 1))

        def _birwkv(r, k, v, w, u):
            wc = w.reshape(-1)
            uc = u.reshape(-1)
            ew = jnp.exp(wc)
            ek = jnp.exp(k)
            Af, Bf = _wkv_scan(ek, v, ew)
            Ab, Bb = _wkv_scan(ek[:, ::-1], v[:, ::-1], ew)
            Ab = Ab[:, ::-1]
            Bb = Bb[:, ::-1]
            cur = jnp.exp(uc + k)
            wkv = (Af + Ab + cur * v) / (Bf + Bb + cur)
            return jax.nn.sigmoid(r) * wkv
        key = jax.random.key(seed)
        k1, k2, k3, k4, k5 = jax.random.split(key, 5)
        r = jax.random.normal(k1, (B_SZ, T_LEN, C_DIM), dtype=jnp.float32)
        k = jax.random.normal(k2, (B_SZ, T_LEN, C_DIM), dtype=jnp.float32)
        v = jax.random.normal(k3, (B_SZ, T_LEN, C_DIM), dtype=jnp.float32)
        w = -(0.3 + jax.random.uniform(k4, (1, 1, C_DIM), dtype=jnp.float32))
        u = jax.random.normal(k5, (1, 1, C_DIM), dtype=jnp.float32) * 0.1
        return {'r': r, 'k': k, 'v': v, 'w': w, 'u': u}
    _L3_xattn_all = _L3_xattn_setup()
    _L3_xattn_in = {k: v for k, v in _L3_xattn_all.items() if k in ('w', 'u')}
    del _L3_xattn_all

    def _L3_ffn_setup():
        import jax, jax.numpy as jnp
        import numpy as np
        B, S, D, E, F = (2, 128, 128, 14, 256)
        key = jax.random.key(seed)
        k0, k1, k2, k3 = jax.random.split(key, 4)
        h = jax.random.normal(k0, (B, S, D), jnp.float32)
        gate_w = jax.random.normal(k1, (E, D), jnp.float32) * 0.02
        w1 = jax.random.normal(k2, (E, D, F), jnp.float32) * (1.0 / np.sqrt(D).astype(np.float32))
        b1 = jnp.zeros((E, F), jnp.float32)
        w2 = jax.random.normal(k3, (E, F, D), jnp.float32) * (1.0 / np.sqrt(F).astype(np.float32))
        b2 = jnp.zeros((E, D), jnp.float32)
        return {'h': h, 'gate_w': gate_w, 'w1': w1, 'b1': b1, 'w2': w2, 'b2': b2}
    _L3_ffn_all = _L3_ffn_setup()
    _L3_ffn_in = {k: v for k, v in _L3_ffn_all.items() if k in ('gate_w', 'w1', 'b1', 'w2', 'b2')}
    del _L3_ffn_all
    return {'x': x, 'ctx_1024': ctx_1024, 'fside_SxS2_0': fside_SxS2_0, 'L0_attn_W_attn': _L0_attn_in['W_attn'], 'L0_attn_W_proj': _L0_attn_in['W_proj'], 'L0_xattn_ifgate_w': _L0_xattn_in['ifgate_w'], 'L0_xattn_ifgate_b': _L0_xattn_in['ifgate_b'], 'L0_xattn_outnorm_w': _L0_xattn_in['outnorm_w'], 'L0_ffn_w_gate': _L0_ffn_in['w_gate'], 'L0_ffn_w_noise': _L0_ffn_in['w_noise'], 'L0_ffn_Wd': _L0_ffn_in['Wd'], 'L0_ffn_bd': _L0_ffn_in['bd'], 'L0_ffn_Wu': _L0_ffn_in['Wu'], 'L0_ffn_bu': _L0_ffn_in['bu'], 'L1_attn_rotation_params': _L1_attn_in['rotation_params'], 'L1_attn_entangle_params': _L1_attn_in['entangle_params'], 'L1_xattn_ln_g': _L1_xattn_in['ln_g'], 'L1_xattn_ln_b': _L1_xattn_in['ln_b'], 'L1_xattn_cln_g': _L1_xattn_in['cln_g'], 'L1_xattn_cln_b': _L1_xattn_in['cln_b'], 'L1_xattn_Wq': _L1_xattn_in['Wq'], 'L1_xattn_Wkv': _L1_xattn_in['Wkv'], 'L1_xattn_Wo': _L1_xattn_in['Wo'], 'L1_xattn_Wff1': _L1_xattn_in['Wff1'], 'L1_xattn_Wff2': _L1_xattn_in['Wff2'], 'L1_ffn_W1': _L1_ffn_in['W1'], 'L1_ffn_b1': _L1_ffn_in['b1'], 'L1_ffn_W2': _L1_ffn_in['W2'], 'L1_ffn_b2': _L1_ffn_in['b2'], 'L1_ffn_scale': _L1_ffn_in['scale'], 'L2_attn_W_in': _L2_attn_in['W_in'], 'L2_attn_conv_w': _L2_attn_in['conv_w'], 'L2_attn_conv_b': _L2_attn_in['conv_b'], 'L2_attn_W_x': _L2_attn_in['W_x'], 'L2_attn_W_dt': _L2_attn_in['W_dt'], 'L2_attn_b_dt': _L2_attn_in['b_dt'], 'L2_attn_A_log': _L2_attn_in['A_log'], 'L2_attn_D_param': _L2_attn_in['D_param'], 'L2_attn_W_out': _L2_attn_in['W_out'], 'L2_xattn_W_q': _L2_xattn_in['W_q'], 'L2_xattn_W_k': _L2_xattn_in['W_k'], 'L2_xattn_W_v': _L2_xattn_in['W_v'], 'L2_xattn_W_out': _L2_xattn_in['W_out'], 'L2_xattn_b_out': _L2_xattn_in['b_out'], 'L2_ffn_w_gate': _L2_ffn_in['w_gate'], 'L2_ffn_w_up': _L2_ffn_in['w_up'], 'L2_ffn_w_down': _L2_ffn_in['w_down'], 'L3_attn_Wq': _L3_attn_in['Wq'], 'L3_attn_bq': _L3_attn_in['bq'], 'L3_attn_Wk': _L3_attn_in['Wk'], 'L3_attn_bk': _L3_attn_in['bk'], 'L3_attn_Wv': _L3_attn_in['Wv'], 'L3_attn_bv': _L3_attn_in['bv'], 'L3_attn_Wo': _L3_attn_in['Wo'], 'L3_attn_bo': _L3_attn_in['bo'], 'L3_attn_alpha': _L3_attn_in['alpha'], 'L3_attn_aug_param': _L3_attn_in['aug_param'], 'L3_attn_ln_scale': _L3_attn_in['ln_scale'], 'L3_attn_ln_bias': _L3_attn_in['ln_bias'], 'L3_xattn_w': _L3_xattn_in['w'], 'L3_xattn_u': _L3_xattn_in['u'], 'L3_ffn_gate_w': _L3_ffn_in['gate_w'], 'L3_ffn_w1': _L3_ffn_in['w1'], 'L3_ffn_b1': _L3_ffn_in['b1'], 'L3_ffn_w2': _L3_ffn_in['w2'], 'L3_ffn_b2': _L3_ffn_in['b2']}

def reference(x, ctx_1024, fside_SxS2_0, L0_attn_W_attn, L0_attn_W_proj, L0_xattn_ifgate_w, L0_xattn_ifgate_b, L0_xattn_outnorm_w, L0_ffn_w_gate, L0_ffn_w_noise, L0_ffn_Wd, L0_ffn_bd, L0_ffn_Wu, L0_ffn_bu, L1_attn_rotation_params, L1_attn_entangle_params, L1_xattn_ln_g, L1_xattn_ln_b, L1_xattn_cln_g, L1_xattn_cln_b, L1_xattn_Wq, L1_xattn_Wkv, L1_xattn_Wo, L1_xattn_Wff1, L1_xattn_Wff2, L1_ffn_W1, L1_ffn_b1, L1_ffn_W2, L1_ffn_b2, L1_ffn_scale, L2_attn_W_in, L2_attn_conv_w, L2_attn_conv_b, L2_attn_W_x, L2_attn_W_dt, L2_attn_b_dt, L2_attn_A_log, L2_attn_D_param, L2_attn_W_out, L2_xattn_W_q, L2_xattn_W_k, L2_xattn_W_v, L2_xattn_W_out, L2_xattn_b_out, L2_ffn_w_gate, L2_ffn_w_up, L2_ffn_w_down, L3_attn_Wq, L3_attn_bq, L3_attn_Wk, L3_attn_bk, L3_attn_Wv, L3_attn_bv, L3_attn_Wo, L3_attn_bo, L3_attn_alpha, L3_attn_aug_param, L3_attn_ln_scale, L3_attn_ln_bias, L3_xattn_w, L3_xattn_u, L3_ffn_gate_w, L3_ffn_w1, L3_ffn_b1, L3_ffn_w2, L3_ffn_b2):
    import jax
    import jax.numpy as jnp

    def _L0_attn_ref(x, W_attn, W_proj):
        import jax, jax.numpy as jnp
        import numpy as np
        import math
        N_HEAD = 16
        HEAD_QKV = 128
        WM_DECAY_LENGTH = 256
        WM_DECAY_RATE = 1.0
        WM_ECHOIC = 16

        def decay_weight_matrix(n):
            dl = WM_DECAY_LENGTH - WM_ECHOIC + 1
            nums = jnp.linspace(0.0, 1.0, dl)
            decay_values = 1.0 - jnp.power(nums, 1.0 / (np.e * WM_DECAY_RATE))
            decay_values = jnp.concatenate([jnp.ones(WM_ECHOIC - 1), decay_values])
            decay_values = decay_values[:n]
            idx = jnp.arange(n)[:, None] - jnp.arange(n)[None, :]
            mat = decay_values[jnp.clip(idx, 0, n - 1)]
            return jnp.tril(mat).astype(jnp.float32)
        B, T, C = x.shape
        hd = HEAD_QKV // N_HEAD
        qkv = x @ W_attn
        q, k, v = jnp.split(qkv, 3, axis=-1)
        q = q.reshape(B, T, N_HEAD, hd).transpose(0, 2, 1, 3)
        k = k.reshape(B, T, N_HEAD, hd).transpose(0, 2, 1, 3)
        v = v.reshape(B, T, N_HEAD, hd).transpose(0, 2, 1, 3)
        att = jnp.einsum('bhqd,bhkd->bhqk', q, k) * (1.0 / math.sqrt(hd))
        causal = jnp.tril(jnp.ones((T, T), dtype=bool))
        att = jnp.where(causal, att, -jnp.inf)
        att = jax.nn.softmax(att, axis=-1)
        att = att * decay_weight_matrix(T)
        y = jnp.einsum('bhqk,bhkd->bhqd', att, v)
        y = y.transpose(0, 2, 1, 3).reshape(B, T, HEAD_QKV)
        return y @ W_proj

    def _L0_xattn_ref(q, k, v, ifgate_w, ifgate_b, outnorm_w):
        import jax, jax.numpy as jnp
        import numpy as np
        B, S, DIM, NH = (2, 256, 128, 8)
        DH = DIM // NH
        GATE_SOFT_CAP = 15.0
        BACKEND_EPS = 5e-05
        NORM_EPS = 1e-06

        def _mlstm_parallel(q, k, v, i_pre, f_pre):
            log_fg = jax.nn.log_sigmoid(f_pre)
            lf_cs = jnp.cumsum(log_fg, axis=-1)
            lf = jnp.concatenate([jnp.zeros_like(lf_cs[..., :1]), lf_cs], axis=-1)
            log_d = lf[..., 1:, None] - lf[..., None, 1:] + i_pre[..., None, :]
            t_idx = jnp.arange(q.shape[2])
            mask = t_idx[:, None] >= t_idx[None, :]
            log_d = jnp.where(mask, log_d, -jnp.inf)
            m = jnp.max(log_d, axis=-1, keepdims=True)
            d_mat = jnp.exp(log_d - m)
            scores = jnp.einsum('bhtd,bhsd->bhts', q, k) * (1.0 / np.sqrt(DH))
            s_mat = scores * d_mat
            denom = jnp.maximum(jnp.abs(jnp.sum(s_mat, axis=-1, keepdims=True)), jnp.exp(-m)) + BACKEND_EPS
            return jnp.einsum('bhts,bhsd->bhtd', s_mat, v) / denom
        b, s, dim = q.shape
        gate_in = jnp.concatenate([q, k, v], axis=-1)
        pre = gate_in @ ifgate_w.T + ifgate_b
        pre = GATE_SOFT_CAP * jnp.tanh(pre / GATE_SOFT_CAP)
        i_pre = pre[..., :NH].transpose(0, 2, 1)
        f_pre = pre[..., NH:].transpose(0, 2, 1)
        qh = q.reshape(b, s, NH, DH).transpose(0, 2, 1, 3)
        kh = k.reshape(b, s, NH, DH).transpose(0, 2, 1, 3)
        vh = v.reshape(b, s, NH, DH).transpose(0, 2, 1, 3)
        h = _mlstm_parallel(qh, kh, vh, i_pre, f_pre)
        rrms = jax.lax.rsqrt(jnp.mean(h * h, axis=-1, keepdims=True) + NORM_EPS)
        gain = (1.0 + outnorm_w).reshape(1, NH, 1, DH)
        h = h * rrms * gain
        return h.transpose(0, 2, 1, 3).reshape(b, s, dim)

    def _L0_ffn_ref(x, w_gate, w_noise, Wd, bd, Wu, bu):
        import jax, jax.numpy as jnp
        import numpy as np
        D_MODEL = 128
        N_EXPERTS = 8
        TOP_K = 2
        BOTTLENECK = 64
        B, S = (2, 512)
        ADAPTER_SCALE = 0.5

        def _moe_forward(x, w_gate, w_noise, Wd, bd, Wu, bu):
            b, s, d = x.shape
            xf = x.reshape(-1, d)
            T = xf.shape[0]
            clean_logits = xf @ w_gate
            logits = clean_logits
            k1 = min(TOP_K + 1, N_EXPERTS)
            top_logits, top_idx = jax.lax.top_k(logits, k1)
            top_k_logits = top_logits[:, :TOP_K]
            top_k_idx = top_idx[:, :TOP_K]
            top_k_gates = jax.nn.softmax(top_k_logits, axis=-1)
            rows = jnp.arange(T)[:, None]
            gates = jnp.zeros((T, N_EXPERTS), dtype=top_k_gates.dtype)
            gates = gates.at[rows, top_k_idx].set(top_k_gates)
            h = jax.nn.relu(jnp.einsum('td,edb->teb', xf, Wd) + bd[None, :, :])
            y = jnp.einsum('teb,ebd->ted', h, Wu) + bu[None, :, :]
            y = ADAPTER_SCALE * y
            out = jnp.einsum('te,ted->td', gates, y)
            return out.reshape(b, s, d)
        return _moe_forward(x, w_gate, w_noise, Wd, bd, Wu, bu)

    def _L1_attn_ref(inputs, rotation_params, entangle_params):
        import jax, jax.numpy as jnp
        import numpy as np
        EMBED_DIM = 128
        NUM_HEADS = 16
        HEAD_DIM = EMBED_DIM // NUM_HEADS
        B, T, _ = inputs.shape
        x = inputs.reshape(B, T, NUM_HEADS, HEAD_DIM).transpose(0, 2, 1, 3)
        q = x * rotation_params[None, :, None, :]
        k = x * entangle_params[None, :, None, :]
        v = x
        scale = 1.0 / np.sqrt(HEAD_DIM).astype(np.float32)
        attn_scores = jnp.einsum('bhid,bhjd->bhij', q, k) * scale
        attn_weights = jax.nn.softmax(attn_scores, axis=-1)
        out = jnp.einsum('bhij,bhjd->bhid', attn_weights, v)
        out = out.transpose(0, 2, 1, 3).reshape(B, T, EMBED_DIM)
        return out

    def _L1_xattn_ref(x, context, ln_g, ln_b, cln_g, cln_b, Wq, Wkv, Wo, Wff1, Wff2):
        import jax, jax.numpy as jnp
        import numpy as np
        DIM = 128
        CTX_DIM = 128
        HEADS = 16
        DIM_HEAD = 64
        INNER = HEADS * DIM_HEAD
        FF_INNER = 4 * DIM
        EPS = 1e-05

        def layer_norm(x, g, b):
            mu = jnp.mean(x, axis=-1, keepdims=True)
            var = jnp.var(x, axis=-1, keepdims=True)
            return (x - mu) * jax.lax.rsqrt(var + EPS) * g + b
        scale = DIM_HEAD ** (-0.5)
        xn = layer_norm(x, ln_g, ln_b)
        cn = layer_norm(context, cln_g, cln_b)
        b, n, _ = xn.shape
        q = (xn @ Wq).reshape(b, n, HEADS, DIM_HEAD).transpose(0, 2, 1, 3) * scale
        kv = cn @ Wkv
        k, v = (kv[..., :DIM_HEAD], kv[..., DIM_HEAD:])
        sim = jnp.einsum('bhid,bjd->bhij', q, k)
        attn = jax.nn.softmax(sim, axis=-1)
        out = jnp.einsum('bhij,bjd->bhid', attn, v)
        out = out.transpose(0, 2, 1, 3).reshape(b, n, INNER) @ Wo
        ff = xn @ Wff1
        h, gate = (ff[..., :FF_INNER], ff[..., FF_INNER:])
        out = out + jax.nn.silu(gate) * h @ Wff2
        return out

    def _L1_ffn_ref(x, W1, b1, W2, b2, scale):
        import jax, jax.numpy as jnp
        import numpy as np
        LORA_DIM = 16
        LORA_TOKEN_INDEX = 1
        B, S, D, H = (4, 256, 128, 512)
        Bx, Sx, Dx = x.shape
        Hx = W1.shape[0]
        lt = jax.lax.dynamic_slice_in_dim(x, LORA_TOKEN_INDEX, LORA_DIM, axis=1)
        even = lt[:, ::2, :]
        odd = lt[:, 1::2, :]
        m1 = (even[:, :4, :, None] * odd[:, :4, None, :]).reshape(Bx, Hx, Dx)
        m2 = (even[:, 4:, :, None] * odd[:, 4:, None, :]).reshape(Bx, Dx, Hx)
        h = jnp.einsum('bsd,hd->bsh', x, W1) + scale * jnp.einsum('bsd,bhd->bsh', x, m1) + b1
        h = jax.nn.gelu(h, approximate=False)
        out = jnp.einsum('bsh,oh->bso', h, W2) + scale * jnp.einsum('bsh,boh->bso', h, m2) + b2
        return out

    def _L2_attn_ref(x, W_in, conv_w, conv_b, W_x, W_dt, b_dt, A_log, D_param, W_out):
        import jax, jax.numpy as jnp
        import numpy as np
        from jax import lax
        D_MODEL = 128
        D_INNER = 2 * D_MODEL
        D_STATE = 16
        D_CONV = 4
        DT_RANK = 64
        DT_MIN = 0.001
        DT_MAX = 0.1
        BATCH = 4
        SEQ = 256
        xz = x @ W_in
        x_branch, z_branch = jnp.split(xz, 2, axis=-1)
        xc = jnp.pad(x_branch.transpose(0, 2, 1), ((0, 0), (0, 0), (D_CONV - 1, 0)))
        xc = lax.conv_general_dilated(xc, conv_w, (1,), 'VALID', dimension_numbers=('NCH', 'OIH', 'NCH'), feature_group_count=D_INNER)
        xc = xc + conv_b[None, :, None]
        x_conv = jax.nn.silu(xc.transpose(0, 2, 1))
        x_dbl = x_conv @ W_x
        dt_low = x_dbl[..., :DT_RANK]
        Bm = x_dbl[..., DT_RANK:DT_RANK + D_STATE]
        Cm = x_dbl[..., DT_RANK + D_STATE:]
        dt = jax.nn.sigmoid(dt_low @ W_dt + b_dt) * (DT_MAX - DT_MIN) + DT_MIN
        dt = jnp.maximum(dt, 0.0001)
        A = -jnp.exp(A_log)

        def step(h, inp):
            dt_t, B_t, C_t, x_t = inp
            dA = jnp.exp(dt_t[:, :, None] * A[None])
            h = dA * h + (dt_t * x_t)[:, :, None] * B_t[:, None, :]
            y_t = jnp.sum(h * C_t[:, None, :], axis=-1)
            return (h, y_t)
        h0 = jnp.zeros((x.shape[0], D_INNER, D_STATE), dtype=x.dtype)
        _, ys = lax.scan(step, h0, (dt.swapaxes(0, 1), Bm.swapaxes(0, 1), Cm.swapaxes(0, 1), x_conv.swapaxes(0, 1)))
        y = ys.swapaxes(0, 1)
        y = y + x_conv * D_param
        y = y * jax.nn.silu(z_branch)
        return y @ W_out

    def _L2_xattn_ref(x, context, bias, W_q, W_k, W_v, W_out, b_out):
        import jax, jax.numpy as jnp
        import numpy as np
        D_MODEL, D_HEAD, N_HEAD = (128, 64, 16)
        B, T1, T2 = (2, 256, 256)
        Bq, T1_, _ = x.shape
        T2_ = context.shape[1]
        atten_scale = 1.0 / np.sqrt(D_HEAD)
        head_scale = jnp.exp2(-jnp.arange(1, N_HEAD + 1, dtype=jnp.float32))
        q = (x @ W_q).reshape(Bq, T1_, N_HEAD, D_HEAD).transpose(0, 2, 1, 3)
        k = (context @ W_k).reshape(Bq, T2_, N_HEAD, D_HEAD).transpose(0, 2, 1, 3)
        v = (context @ W_v).reshape(Bq, T2_, N_HEAD, D_HEAD).transpose(0, 2, 1, 3)
        scores = jnp.einsum('bhqd,bhkd->bhqk', q, k) * atten_scale
        scores = scores + bias[None, None, :, :] * head_scale[None, :, None, None]
        attn = jax.nn.softmax(scores, axis=-1)
        out = jnp.einsum('bhqk,bhkd->bqhd', attn, v).reshape(Bq, T1_, N_HEAD * D_HEAD)
        return out @ W_out + b_out

    def _L2_ffn_ref(x, w_gate, w_up, w_down):
        import jax, jax.numpy as jnp
        import numpy as np
        BLOCK = 16
        _GRID = jnp.array([0.0, 0.5, 1.0, 1.5, 2.0, 3.0, 4.0, 6.0], dtype=jnp.float32)
        _MID = jnp.array([0.25, 0.75, 1.25, 1.75, 2.5, 3.5, 5.0], dtype=jnp.float32)

        def fp4_quant_dequant(x):
            shape = x.shape
            xb = x.reshape(shape[:-1] + (shape[-1] // BLOCK, BLOCK))
            scale = jnp.max(jnp.abs(xb), axis=-1, keepdims=True) / 6.0
            scale = jnp.maximum(scale, jnp.float32(1e-12))
            xn = xb / scale
            idx = jnp.searchsorted(_MID, jnp.abs(xn))
            q = _GRID[idx] * jnp.sign(xn) * scale
            return q.reshape(shape)

        def fp4_linear(x, w):
            xq = fp4_quant_dequant(x)
            wq = fp4_quant_dequant(w)
            return jnp.einsum('bsk,nk->bsn', xq, wq)
        gate = fp4_linear(x, w_gate)
        y = fp4_linear(x, w_up)
        h = jax.nn.silu(gate) * y
        return fp4_linear(h, w_down)

    def _L3_attn_ref(x, Wq, bq, Wk, bk, Wv, bv, Wo, bo, alpha, aug_param, ln_scale, ln_bias):
        import jax, jax.numpy as jnp
        import numpy as np
        HIDDEN, HEADS, HDIM = (128, 8, 64)
        B, S = (4, 1024)
        LN_EPS = 1e-06
        b, s, _ = x.shape
        h, d = alpha.shape
        scale = d ** (-0.5)
        q = (x @ Wq + bq).reshape(b, s, h, d)
        k = (x @ Wk + bk).reshape(b, s, h, d)
        v = (x @ Wv + bv).reshape(b, s, h, d)
        decay = jax.nn.sigmoid(alpha)

        def step(state, qkv):
            q_t, k_t, v_t = qkv
            attn = jax.nn.softmax(jnp.einsum('bhd,bhd->bh', q_t, k_t) * scale, axis=-1)
            new_state = decay * state + (1.0 - decay) * attn[..., None] * v_t
            return (new_state, new_state)
        qs = jnp.moveaxis(q, 1, 0)
        ks_ = jnp.moveaxis(k, 1, 0)
        vs = jnp.moveaxis(v, 1, 0)
        init = jnp.zeros((b, h, d), x.dtype)
        _, states = jax.lax.scan(step, init, (qs, ks_, vs))
        states = jnp.moveaxis(states, 0, 1)
        aug = jax.nn.sigmoid(q * aug_param)
        out = (q * states + aug).reshape(b, s, h * d)
        out = out @ Wo + bo
        mean = jnp.mean(out, axis=-1, keepdims=True)
        var = jnp.var(out, axis=-1, keepdims=True)
        return (out - mean) * jax.lax.rsqrt(var + LN_EPS) * ln_scale + ln_bias

    def _L3_xattn_ref(r, k, v, w, u):
        import jax, jax.numpy as jnp
        import numpy as np
        B_SZ, T_LEN, C_DIM = (4, 512, 128)

        def _wkv_scan(ek, v, ew):

            def step(carry, xt):
                A, Bd = carry
                ekt, vt = xt
                out = (A, Bd)
                A2 = ew * A + ekt * vt
                B2 = ew * Bd + ekt
                return ((A2, B2), out)
            init = (jnp.zeros_like(ek[:, 0]), jnp.zeros_like(ek[:, 0]))
            xs = (jnp.moveaxis(ek, 1, 0), jnp.moveaxis(v, 1, 0))
            _, (A, Bd) = jax.lax.scan(step, init, xs)
            return (jnp.moveaxis(A, 0, 1), jnp.moveaxis(Bd, 0, 1))

        def _birwkv(r, k, v, w, u):
            wc = w.reshape(-1)
            uc = u.reshape(-1)
            ew = jnp.exp(wc)
            ek = jnp.exp(k)
            Af, Bf = _wkv_scan(ek, v, ew)
            Ab, Bb = _wkv_scan(ek[:, ::-1], v[:, ::-1], ew)
            Ab = Ab[:, ::-1]
            Bb = Bb[:, ::-1]
            cur = jnp.exp(uc + k)
            wkv = (Af + Ab + cur * v) / (Bf + Bb + cur)
            return jax.nn.sigmoid(r) * wkv
        return _birwkv(r, k, v, w, u)

    def _L3_ffn_ref(h, gate_w, w1, b1, w2, b2):
        import jax, jax.numpy as jnp
        import numpy as np
        B, S, D, E, F = (2, 128, 128, 14, 256)
        Bb, Ss, Dd = h.shape
        x = h.reshape(Bb * Ss, Dd)
        logits = x @ gate_w.T
        probs = jax.nn.softmax(logits, axis=-1)
        top2_p, top2_i = jax.lax.top_k(probs, 2)
        w = top2_p / jnp.maximum(top2_p.sum(-1, keepdims=True), 1e-10)
        hh = jnp.einsum('nd,edf->nef', x, w1) + b1
        hh = jax.nn.gelu(hh, approximate=False)
        all_out = jnp.einsum('nef,efd->ned', hh, w2) + b2
        n = jnp.arange(x.shape[0])
        out0 = all_out[n, top2_i[:, 0]]
        out1 = all_out[n, top2_i[:, 1]]
        moe_out = w[:, 0:1] * out0 + w[:, 1:2] * out1
        result = jnp.clip(x + moe_out, -100.0, 100.0).reshape(Bb, Ss, Dd)
        return result
    x = x + _L0_attn_ref(_layernorm(x, axis=-1), L0_attn_W_attn, L0_attn_W_proj)
    x = x + _L0_xattn_ref(_layernorm(x, axis=-1), ctx_1024, ctx_1024, L0_xattn_ifgate_w, L0_xattn_ifgate_b, L0_xattn_outnorm_w)
    x = x + _L0_ffn_ref(_layernorm(x, axis=-1), L0_ffn_w_gate, L0_ffn_w_noise, L0_ffn_Wd, L0_ffn_bd, L0_ffn_Wu, L0_ffn_bu)
    x = x + _L1_attn_ref(_layernorm(x, axis=-1), L1_attn_rotation_params, L1_attn_entangle_params)
    x = x + _L1_xattn_ref(_layernorm(x, axis=-1), ctx_1024, L1_xattn_ln_g, L1_xattn_ln_b, L1_xattn_cln_g, L1_xattn_cln_b, L1_xattn_Wq, L1_xattn_Wkv, L1_xattn_Wo, L1_xattn_Wff1, L1_xattn_Wff2)
    x = x + _L1_ffn_ref(_layernorm(x, axis=-1), L1_ffn_W1, L1_ffn_b1, L1_ffn_W2, L1_ffn_b2, L1_ffn_scale)
    x = x + _L2_attn_ref(_layernorm(x, axis=-1), L2_attn_W_in, L2_attn_conv_w, L2_attn_conv_b, L2_attn_W_x, L2_attn_W_dt, L2_attn_b_dt, L2_attn_A_log, L2_attn_D_param, L2_attn_W_out)
    x = x + _L2_xattn_ref(_layernorm(x, axis=-1), ctx_1024, fside_SxS2_0, L2_xattn_W_q, L2_xattn_W_k, L2_xattn_W_v, L2_xattn_W_out, L2_xattn_b_out)
    x = x + _L2_ffn_ref(_layernorm(x, axis=-1), L2_ffn_w_gate, L2_ffn_w_up, L2_ffn_w_down)
    x = x + _L3_attn_ref(_layernorm(x, axis=-1), L3_attn_Wq, L3_attn_bq, L3_attn_Wk, L3_attn_bk, L3_attn_Wv, L3_attn_bv, L3_attn_Wo, L3_attn_bo, L3_attn_alpha, L3_attn_aug_param, L3_attn_ln_scale, L3_attn_ln_bias)
    x = x + _L3_xattn_ref(_layernorm(x, axis=-1), ctx_1024, ctx_1024, L3_xattn_w, L3_xattn_u)
    x = x + _L3_ffn_ref(_layernorm(x, axis=-1), L3_ffn_gate_w, L3_ffn_w1, L3_ffn_b1, L3_ffn_w2, L3_ffn_b2)
    return x

_drawn_inputs = setup_inputs


def setup_inputs(seed=0):
    import zlib

    import numpy as np

    out = dict(_drawn_inputs(seed))
    spreads = {'L0_xattn_outnorm_w': (0.0, 0.1),
     'L0_ffn_bd': (0.0, 0.8),
     'L0_ffn_bu': (0.0, 0.288),
     'L1_xattn_ln_g': (1.0, 0.2),
     'L1_xattn_ln_b': (0.0, 0.1),
     'L1_xattn_cln_g': (1.0, 0.2),
     'L1_xattn_cln_b': (0.0, 0.1),
     'L1_ffn_b1': (0.0, 0.517),
     'L1_ffn_b2': (0.0, 0.1),
     'L2_attn_D_param': (1.0, 0.6),
     'L2_xattn_b_out': (0.0, 0.1),
     'L3_attn_bq': (0.0, 0.335),
     'L3_attn_bk': (0.0, 2.0),
     'L3_attn_bv': (0.0, 0.494),
     'L3_attn_bo': (0.0, 0.1),
     'L3_attn_alpha': (1.0, 0.6),
     'L3_attn_ln_scale': (1.0, 0.2),
     'L3_attn_ln_bias': (0.0, 0.289),
     'L3_ffn_b1': (0.0, 0.63),
     'L3_ffn_b2': (0.0, 0.44)}
    factors = {'L0_ffn_Wd': 6.912,
     'L0_ffn_Wu': 5.62,
     'L2_attn_conv_w': 3.161,
     'L2_attn_conv_b': 3.884,
     'L2_attn_W_x': 8.0,
     'L2_attn_W_dt': 8.0,
     'L2_attn_b_dt': 8.0,
     'L2_attn_A_log': 8.0,
     'L2_ffn_w_gate': 6.844,
     'L2_ffn_w_up': 6.309,
     'L2_ffn_w_down': 6.74,
     'L3_xattn_u': 29.198,
     'L3_xattn_w': 3.651}
    for name, (base, spread) in spreads.items():
        noise = np.random.default_rng([zlib.crc32(name.encode()), seed]).standard_normal(out[name].shape)
        drawn = base * np.exp(spread * noise) if base else spread * noise
        out[name] = jnp.asarray(drawn.astype(out[name].dtype))
    for name, factor in factors.items():
        out[name] = (out[name] * factor).astype(out[name].dtype)
    return out
```

```python
from contextlib import ExitStack

import numpy as np
import concourse.bass as bass
from concourse import mybir
from concourse.alu_op_type import AluOpType as ALU

F32 = mybir.dt.float32
BF16 = mybir.dt.bfloat16
I32 = mybir.dt.int32
ACT = mybir.ActivationFunctionType
AX = mybir.AxisListType

P = 128
NB = 16
D = 128
QUAD = 4
NQ = NB // QUAD
TOK = NB * P
QT = QUAD * P
NEG = -1.0e30

LAYOUT = {
    "const": dict(ident=(128, 128), mask_qk=(128, 128), mask_kq=(128, 128), decay=(128, 128),
                  heads=(128, 16), heads16=(128, 8), sel_e=(8, 512), pairs=(128, 8), rows3=(96, 32)),
    "l0_attn": dict(wq=(128, 128), wk=(128, 128), wv=(128, 128), wo=(128, 128)),
    "l0_mlstm": dict(wg=(128, 48), bias=(128, 2), gain=(128, 128)),
    "l0_moe": dict(wg=(128, 8), wd=(128, 512), bd=(128, 4), wu=(128, 512), bu=(8, 128)),
    "l1_attn": dict(rot=(128, 1), ent=(128, 1)),
    "l1_xattn": dict(ln_g=(128, 1), ln_b=(128, 1), cln_g=(128, 1), cln_b=(128, 1), wq=(128, 1024), wkk=(128, 128),
                     wv=(128, 64), wo=(128, 1024), wff1=(128, 1024), wff2=(128, 512)),
    "l1_ffn": dict(w1=(128, 512), b1=(128, 4), w2=(128, 512), b2=(1, 128), scale=(128, 1)),
    "l2_mamba": dict(w_in=(128, 512), conv_w=(128, 8), conv_b=(128, 2), w_x=(128, 256), w_dt=(128, 256),
                     b_dt=(128, 2), a_log=(128, 32), d_skip=(128, 2), w_out=(128, 256)),
    "l2_xattn": dict(wq=(128, 1024), wk=(128, 1024), wv=(128, 1024), wo=(128, 1024), b_out=(1, 128), bias=(128, 128)),
    "l2_ffn": dict(wg=(128, 384), wu=(128, 384), wd=(128, 352)),
    "l3_attn": dict(wq=(128, 512), wk=(128, 512), wv=(128, 512), bq=(128, 4), bk=(128, 4), bv=(128, 4),
                    wo=(128, 512), bo=(1, 128), alpha=(128, 4), aug=(128, 4), ln_scale=(128, 128),
                    ln_bias=(128, 128), heads=(128, 32)),
    "l3_rwkv": dict(w=(128, 1), u=(128, 1)),
    "l3_moe": dict(gate=(128, 14), w1=(128, 3584), b1=(128, 28), w2=(128, 3584), b2=(14, 128)),
}


EARLY = ("l0_attn", "l0_mlstm", "l0_moe", "l1_attn", "l1_xattn", "l1_ffn")


def spans(group):
    at, out = 0, {}
    for name, (rows, cols) in LAYOUT[group].items():
        out[name] = (rows, at, at + cols)
        at += cols
    return out, at


def whole(x):
    return isinstance(x, int)


def after(eng, sem, value):
    if whole(value) and value <= 0:
        return
    eng.wait_ge(sem, value)


def heads4(ap):
    return ap.rearrange("p (h k) -> p h k", h=4)


def along(ap, shape):
    return ap.unsqueeze(len(ap.shape)).broadcast_to(shape)


def bodies(eng, body):
    body(0, 0)
    with eng.Fori(0, NB // 2 - 1) as i:
        body(i, 1)
        body(i, 2)
    body(0, NB - 1)
    body(0, NB)


class Scope:

    def __init__(self, nc, G, tag):
        self.nc, self.G, self.tag, self.stack, self.sems = nc, G, tag, ExitStack(), []

    def __enter__(self):
        self.stack.__enter__()
        return self

    def __exit__(self, *what):
        self.G.spent += self.sems
        return self.stack.__exit__(*what)

    def sb(self, name, shape, dt=F32):
        return self.stack.enter_context(self.nc.sbuf_tensor(f"{self.tag}_{name}", shape, dt))

    def sem(self, name):
        handle = self.nc.alloc_semaphore(f"{self.tag}_{name}")
        self.sems.append(handle)
        return handle

    def block(self):
        return self.stack.enter_context(self.nc.Block())


def clear_spent(nc, G, sp, spent):
    numbers = sorted(handle.num for handle in spent)
    start = 0
    for n in range(1, len(numbers) + 1):
        if n == len(numbers) or numbers[n] != numbers[n - 1] + 1:
            sp.sem_clear(range(numbers[start], numbers[n - 1] + 1))
            start = n
    G.cleared += spent


class Link:

    def __init__(self, eng, sem, base=0):
        self.eng, self.sem, self.base, self.n = eng, sem, base, 0

    def __call__(self, ins):
        self.n += 1
        ins.then_inc(self.sem, 1)
        self.eng.wait_ge(self.sem, self.base + self.n)

    def note(self, ins):
        self.n += 1
        ins.then_inc(self.sem, 1)

    def catch(self):
        self.eng.wait_ge(self.sem, self.base + self.n)


def row_stats(nc, s, src, eps):
    HALF = NB // 2
    st = s.sb("st", [P, NB, 2, 3])
    small = s.sb("small", [P, 4, NB])
    mean = s.sb("mean", [P, NB])
    ve = s.sb("ve", [P, NB])
    rs = s.sb("rs", [P, NB])
    neg_half = s.sb("neg_half", [P, NB])
    own, ready, rstd, exponent = s.sem("stats_own"), s.sem("var_ready"), s.sem("rstd"), s.sem("exponent")

    def stats_of(dve, half):
        bs = slice(HALF * half, HALF * (half + 1))
        link = Link(dve, own, (HALF + 6) * half)
        for b in range(NB)[bs]:
            link.note(nc.vector.bn_stats(st[:, b, :, :].rearrange("p a c -> p (a c)"), src(b)))
        link.catch()
        both, apart, spread, apart2 = (small[:, n, bs] for n in range(4))
        link.note(nc.vector.tensor_tensor(both, st[:, bs, 0, 1], st[:, bs, 1, 1], ALU.add))
        link.note(nc.vector.tensor_tensor(apart, st[:, bs, 0, 1], st[:, bs, 1, 1], ALU.subtract))
        link(nc.vector.tensor_tensor(spread, st[:, bs, 0, 2], st[:, bs, 1, 2], ALU.add))
        link(nc.vector.tensor_tensor(apart2, apart, apart, ALU.mult))
        link(nc.vector.scalar_tensor_tensor(apart2, apart2, D / 4, spread, ALU.mult, ALU.add))
        nc.vector.tensor_scalar(ve[:, bs], apart2, 1.0 / D, eps, ALU.mult, ALU.add).then_inc(ready, 1)
        link(nc.vector.tensor_scalar(mean[:, bs], both, 0.5, None, ALU.mult))

    def rstd_of(pool, half):
        bs = slice(HALF * half, HALF * (half + 1))
        if half == 0:
            nc.gpsimd.memset(neg_half[:], -0.5).then_inc(exponent, 1)
        pool.wait_ge(exponent, 1)
        pool.wait_ge(ready, half + 1)
        nc.gpsimd.tensor_tensor(rs[:, bs], ve[:, bs], neg_half[:, bs], ALU.pow).then_inc(rstd, 1)

    return mean, rs, rstd, stats_of, rstd_of


def layernorm(nc, G, tag, weights, src=None, outT=None, eps=1e-5, gT=None, bT=None, also=None, fetch=None, more=()):
    src = src or (lambda b: G.x[:, b, :])
    outT = G.xnT if outT is None else outT
    first, G.started = not G.started, True
    spent, G.spent = G.spent, []
    for handle in G.cleared:
        nc.release_semaphore(handle)
    G.cleared = []
    with Scope(nc, G, f"ln_{tag}") as s:
        mean, rs, rstd, stats_of, rstd_of = row_stats(nc, s, src, eps)
        normed, turned, stored = (s.sem(n) for n in ("normed", "turned", "stored"))
        block = s.block()

        @block.sync
        def _(sp):
            if fetch:
                for group in EARLY:
                    sp.wait_ge(G.loaded[group], 16)
                sp.dma_start(G.pack[fetch], G.aps[fetch]).then_inc(G.loaded[fetch], 16)
            clear_spent(nc, G, sp, spent)
            for group in (weights, *more) if weights else ():
                sp.wait_ge(G.loaded[group], 16)

        @block.vector
        def _(dve):
            for half in range(2):
                if first:
                    dve.wait_ge(G.loaded[f"x{half}"], 16)
                stats_of(dve, half)
            for b in range(NB):
                if b % (NB // 2) == 0:
                    dve.wait_ge(rstd, 1 + b // (NB // 2))
                view, dst = src(b), G.xn[:, b, :]
                if len(view.shape) == 3:
                    dst = dst.rearrange("p (h d) -> p h d", h=view.shape[1])
                nc.vector.tensor_scalar(dst, view, mean[:, b:b + 1], rs[:, b:b + 1], ALU.subtract, ALU.mult)\
                  .then_inc(normed, 1)
            if first:
                small_constants(nc, G, dve)
            if also:
                dve.wait_ge(G.loaded[weights], 16)
                also(dve)

        @block.gpsimd
        def _(pool):
            for half in range(2):
                rstd_of(pool, half)

        @block.tensor
        def _(pe):
            if first:
                pe.wait_ge(G.loaded["const"], 16)
            for q in range(NQ):
                pe.wait_ge(normed, QUAD * (q + 1))
                for j in range(QUAD):
                    mm = nc.tensor.transpose(G.ps[:, q, j * P:(j + 1) * P], G.xn[:, q * QUAD + j, :], G.c["ident"])
                mm.then_inc(turned, 1)

        @block.scalar
        def _(act):
            for q in range(NQ):
                act.wait_ge(turned, q + 1)
                dst, bank = outT[:, q * QUAD:(q + 1) * QUAD, :], heads4(G.ps[:, q, :])
                if gT is None:
                    nc.scalar.copy(dst, bank).then_inc(stored, 1)
                else:
                    nc.scalar.activation(dst, bank, ACT.Identity, bias=bT, scale=gT).then_inc(stored, 1)


class Heads:

    def __init__(self, tag, dv, narrow, v_cols, kvT, proj, end, reader, w, q_cols=P, k_cols=P, scale=None, q_scale=None,
                 b_out=None, mask=None, bias=None, on_keys=None):
        self.tag, self.dv, self.narrow = tag, dv, narrow
        self.q_cols, self.k_cols, self.v_cols, self.kvT = q_cols, k_cols, v_cols, kvT
        self.proj, self.end, self.reader, self.w = proj, end, reader, w
        self.scale, self.q_scale, self.b_out = scale, q_scale, b_out
        self.mask, self.bias, self.on_keys = mask, bias, on_keys


def attention(nc, G, cfg):
    HG = 4
    LAG_T, LAG_V = 2, 3
    dv, narrow = cfg.dv, cfg.narrow
    n_proj, n_end = len(cfg.proj), len(cfg.end)
    full = len(cfg.proj) > 3
    wide = dv == 64
    

    with Scope(nc, G, cfg.tag) as s:
        q_sb = s.sb("q", [P, 2, cfg.q_cols])
        k_sb = s.sb("k", [P, 2, cfg.k_cols])
        v_sb = s.sb("v", [P, 2, cfg.v_cols]) if cfg.v_cols else None
        src = s.sb("src", [P, 2, P])
        k_one = s.sb("k_one", [P, 2, 512]) if narrow else None
        biased = s.sb("biased", [P, 2, 512]) if cfg.bias else None
        probs = s.sb("probs", [P, 2, 512])
        probsT = s.sb("probsT", [P, 2, 512])
        neg_max = s.sb("neg_max", [P, 2, 4])
        row_sum = s.sb("row_sum", [P, 2, 16])
        recip = s.sb("recip", [P, 16])
        if wide:
            o_sb = G.xn[:, 0:8, :].rearrange("p c k -> p (c k)")
            oT = G.xn[:, 8:16, :]
        else:
            o_sb = s.sb("o", [P, 16 * dv])[:]
            oT = s.sb("oT", [P, 1, P])[:]
        sem_names = ("src_ready", "k_copied", "k_ready", "scored", "bias_added", "maxed", "exped", "turned", "copied", "summed",
                     "p_made", "e_made", "normed", "own", "added")
        (src_ready, k_copied, k_ready, scored, bias_added, maxed, exped, turned, copied, summed, p_made, e_made,
         normed, own, added) = (s.sem(n) for n in sem_names)
        bank = lambda *ns: [G.ps[:, n, :] for n in ns]
        if narrow:
            S, T, PB, EB = bank(0, 1), bank(2, 3), bank(5, 6), bank(7)
        elif cfg.bias:
            S, T, PB, EB = bank(0), bank(2), bank(3, 6), bank(1, 7)
        else:
            S, T, PB, EB = bank(0, 1), bank(2), bank(3, 6), bank(7)
        O = G.ps[:, 4:6, :].rearrange("p b n -> p (b n)")
        of = lambda banks, t: banks[t % len(banks)]
        p_free = [s.sem(f"p_free{j}") for j in range(len(PB))]
        e_free = [s.sem(f"e_free{j}") for j in range(len(EB))]

        def wait_read(eng, free, per, b, n, banks=None):
            for j in range(len(free)) if banks is None else banks:
                in_bank = lambda m: len(range(j, m, len(free)))
                after(eng, free[j], in_bank(per) * b + in_bank(n))

        def steps(i, k):
            b = 2 * i + k
            n_steps = NB * HG
            for hg in range(HG):
                t = b * HG + hg
                live = lambda u: not whole(u) or 0 <= u < n_steps
                yield hg, t, live

        block = s.block()

        @block.tensor
        def _(pe):
            def head(h):
                step, j = h // 4, h % 4
                half, c = step % 2, 4 * (step // 2) + j
                return slice(64 * half, 64 * half + 64), c, c if full else 0

            def scores(t, hg, slot):
                after(pe, bias_added if cfg.bias else exped, t + 1 - len(S))
                bank = of(S, hg)
                if cfg.mask is not None:
                    nc.tensor.matmul(bank, G.ident_bf[:], cfg.mask, start=True, stop=False)
                if narrow:
                    pe.wait_ge(k_ready, t + 1)
                    mm = nc.tensor.matmul(bank, q_sb[:, slot, :], k_one[:, hg % 2, :], start=cfg.mask is None, stop=True)
                else:
                    for g in range(4):
                        rows, qc, kc = head(4 * hg + g)
                        mm = nc.tensor.matmul(bank[:, g * P:(g + 1) * P], q_sb[rows, slot, qc * P:(qc + 1) * P],
                                              k_sb[rows, slot, kc * P:(kc + 1) * P], start=True, stop=True)
                mm.then_inc(scored, 1)

            def turn(u, hg):
                after(pe, exped, u + 1)
                after(pe, copied, u + 1 - len(T))
                for g in range(4):
                    mm = nc.tensor.transpose(of(T, hg)[:, g * P:(g + 1) * P],
                                             probs[:, hg % 2, g * P:(g + 1) * P], G.c["ident"])
                mm.then_inc(turned, 1)

            def times_v(u, hg, b, slot):
                after(pe, copied, u + 1)
                if hg == 0:
                    after(pe, normed, b)
                for g in range(4):
                    h = 4 * hg + g
                    if cfg.v_cols == 0:
                        v = G.xn[:, b, h * dv:(h + 1) * dv]
                    elif cfg.v_cols == 64:
                        v = v_sb[:, slot, :]
                    else:
                        v = v_sb[:, slot, h * dv:(h + 1) * dv]
                    mm = nc.tensor.matmul(O[:, h * dv:(h + 1) * dv], probsT[:, hg % 2, g * P:(g + 1) * P], v,
                                          start=True, stop=True)
                mm.then_inc(summed, 1)

            def project(n, b, slot):
                name, bank = cfg.proj[n][0], of(PB, n)
                wait_read(pe, p_free, n_proj, b, n, [n % len(PB)])
                if name == "qk":
                    tokens = cfg.kvT[:, b, :]
                    nc.tensor.matmul(bank[:, 0:P], cfg.w["q"], tokens, start=True, stop=True)
                    mm = nc.tensor.matmul(bank[:, P:2 * P], cfg.w["k"], tokens, start=True, stop=True)
                elif name in ("q0", "q1", "k0", "k1"):
                    w = cfg.w[name[0]]
                    tokens = G.xnT if name[0] == "q" else cfg.kvT
                    c0 = 4 * int(name[1])
                    for c in range(4):
                        mm = nc.tensor.matmul(bank[:, c * P:(c + 1) * P], w[:, (c0 + c) * P:(c0 + c + 1) * P],
                                              tokens[:, b, :], start=True, stop=True)
                elif name == "kv":
                    nc.tensor.matmul(bank[:, 0:P], cfg.w["k"], cfg.kvT[:, b, :], start=True, stop=True)
                    pe.wait_ge(src_ready, b + 1)
                    mm = nc.tensor.matmul(bank[:, P:P + dv], src[:, slot, :], cfg.w["v"], start=True, stop=True)
                else:
                    c0, n_cols = (0, P) if name == "v" else (512 * int(name[1]), 512)
                    pe.wait_ge(src_ready, b + 1)
                    mm = nc.tensor.matmul(bank[:, 0:n_cols], src[:, slot, :], cfg.w["v"][:, c0:c0 + n_cols],
                                          start=True, stop=True)
                mm.then_inc(p_made, 1)

            def finish(n, b):
                name, bank = cfg.end[n][0], of(EB, n)
                if n == 0:
                    pe.wait_ge(normed, b + 1)
                wait_read(pe, e_free, n_end, b, n, [n % len(EB)])
                if name[0] == "t":
                    c0 = 4 * int(name[1])
                    for c in range(min(4, 16 * dv // P)):
                        mm = nc.tensor.transpose(bank[:, c * P:(c + 1) * P], o_sb[:, (c0 + c) * P:(c0 + c + 1) * P],
                                                 G.c["ident"])
                else:
                    wait_read(pe, e_free, n_end, b, n)
                    chunks = 16 * dv // P
                    for c in range(chunks):
                        mm = nc.tensor.matmul(bank[:, 0:P], oT[:, c, :], cfg.w["o"][:, c * P:(c + 1) * P],
                                              start=c == 0, stop=c == chunks - 1 and cfg.b_out is None)
                    if cfg.b_out is not None:
                        mm = nc.tensor.matmul(bank[:, 0:P], G.c["ones_row"], cfg.b_out, start=False, stop=True)
                mm.then_inc(e_made, 1)

            def pieces(i, k, hg, t, live, place):
                b, slot = 2 * i + k, k % 2
                for n, (_, *at) in enumerate(cfg.proj):
                    if live(t + HG) and at == [hg, place]:
                        project(n, b + 1, 1 - slot)
                for n, (_, *at) in enumerate(cfg.end):
                    if live(t - HG) and at == [hg, place]:
                        finish(n, b - 1)

            def body(i, k):
                b, slot = 2 * i + k, k % 2
                for hg, t, live in steps(i, k):
                    if live(t):
                        if hg == 0 and n_proj:
                            wait_read(pe, p_free, n_proj, b + 1, 0)
                        if hg == 0 and cfg.q_scale is not None:
                            pe.wait_ge(src_ready, b + 1)
                        scores(t, hg, slot)
                    pieces(i, k, hg, t, live, 0)
                    if live(t - LAG_T):
                        turn(t - LAG_T, (hg - LAG_T) % HG)
                    pieces(i, k, hg, t, live, 1)
                    if live(t - LAG_V):
                        u_hg = (hg - LAG_V) % HG
                        u_b, u_slot = (b, slot) if hg >= LAG_V else (b - 1, 1 - slot)
                        times_v(t - LAG_V, u_hg, u_b, u_slot)
                    pieces(i, k, hg, t, live, 2)

            for n in range(n_proj):
                project(n, 0, 0)
            bodies(pe, body)

        def empties(eng, me, i, k, hg, live, t, *places):
            b, slot = 2 * i + k, k % 2
            if live(t + HG):
                for n, (name, *at) in enumerate(cfg.proj):
                    if at[0] == hg and at[1] in places and me in cfg.reader[name]:
                        take_projected(eng, me, n, b + 1, 1 - slot)
            if live(t - HG):
                for n, (name, *at) in enumerate(cfg.end):
                    if at[0] == hg and at[1] in places and me in cfg.reader[name]:
                        take_end(eng, me, n, b - 1)

        def take_end(eng, me, n, b):
            name, bank = cfg.end[n][0], of(EB, n)
            eng.wait_ge(e_made, n_end * b + n + 1)
            if name == "p":
                nc.vector.tensor_tensor(G.x[:, b, :], G.x[:, b, :], bank[:, 0:P], ALU.add).then_inc(of(e_free, n), 1)
            else:
                c0, n_c = 4 * int(name[1]), min(4, 16 * dv // P)
                copy = nc.scalar.copy if me == "A" else nc.vector.tensor_copy
                copy(oT[:, c0:c0 + n_c, :].rearrange("p c k -> p (c k)"), bank[:, 0:n_c * P])\
                    .then_inc(of(e_free, n), 1)

        def take_projected(eng, me, n, b, slot):
            name, bank = cfg.proj[n][0], of(PB, n)
            copy = nc.scalar.copy if me == "A" else nc.vector.tensor_copy
            eng.wait_ge(p_made, n_proj * b + n + 1)
            if name == "kv":
                copy(k_sb[:, slot, :], bank[:, 0:P])
                ins = copy(v_sb[:, slot, :], bank[:, P:P + dv])
            elif name == "qk":
                nc.scalar.activation(q_sb[:, slot, :], bank[:, 0:P], ACT.Copy, scale=cfg.scale)
                ins = copy(k_sb[:, slot, :], bank[:, P:2 * P])
            elif name == "v":
                ins = copy(v_sb[:, slot, :], bank[:, 0:P])
            else:
                c0 = 512 * int(name[1])
                if name[0] == "q" and me == "A":
                    ins = nc.scalar.activation(q_sb[:, slot, c0:c0 + 512], bank, ACT.Copy, scale=cfg.scale)
                else:
                    ins = copy((v_sb if name[0] == "v" else k_sb)[:, slot, c0:c0 + 512], bank)
            ins.then_inc(of(p_free, n), 1)

        @block.vector
        def _(dve):
            def body(i, k):
                b, slot = 2 * i + k, k % 2
                for hg, t, live in steps(i, k):
                    if live(t):
                        dve.wait_ge(scored, t + 1)
                        after(dve, exped, t - 1)
                        values = of(S, hg)
                        if cfg.bias:
                            values = biased[:, hg % 2, :]
                            nc.vector.tensor_tensor(values, of(S, hg), cfg.bias(hg), ALU.add).then_inc(bias_added, 1)
                            dve.wait_ge(bias_added, t + 1)
                        nc.vector.tensor_reduce(neg_max[:, hg % 2, :], heads4(values), AX.X, ALU.max,
                                                negate=True).then_inc(maxed, 1)
                    empties(dve, "V", i, k, hg, live, t, 0)
                    if live(t - LAG_T):
                        u, par = t - LAG_T, (hg - LAG_T) % 2
                        dve.wait_ge(turned, u + 1)
                        after(dve, summed, u - 1)
                        if cfg.on_keys is not None:
                            nc.vector.tensor_tensor(heads4(probsT[:, par, :]), heads4(of(T, par)),
                                                    cfg.on_keys.unsqueeze(1).broadcast_to([P, 4, P]), ALU.mult)\
                              .then_inc(copied, 1)
                        else:
                            nc.vector.tensor_copy(probsT[:, par, :], of(T, par)).then_inc(copied, 1)
                    if hg == LAG_V - 1 and live(t - HG):
                        dve.wait_ge(summed, HG * b)
                        dve.wait_ge(exped, HG * b)
                        nc.vector.reciprocal(recip[:], row_sum[:, 1 - slot, :]).then_inc(own, 1)
                        dve.wait_ge(own, b)
                        if n_end:
                            after(dve, e_made, n_end * (b - 1))
                        for half in range(2 if wide else 1):
                            hs = 8 if wide else 16
                            sl = slice(half * 512, half * 512 + hs * dv)
                            ins = nc.vector.tensor_tensor(
                                o_sb[:, sl].rearrange("p (h d) -> p h d", d=dv),
                                O[:, sl].rearrange("p (h d) -> p h d", d=dv),
                                along(recip[:, half * 8:half * 8 + hs], [P, hs, dv]), ALU.mult)
                        ins.then_inc(normed, 1)
                        if not n_end:
                            dve.wait_ge(normed, b)
                            nc.vector.tensor_tensor(G.x[:, b - 1, :], G.x[:, b - 1, :], o_sb, ALU.add)\
                              .then_inc(added, 1)
                    empties(dve, "V", i, k, hg, live, t, 1, 2)

            for n, (name, _, _) in enumerate(cfg.proj):
                if "V" in cfg.reader[name]:
                    take_projected(dve, "V", n, 0, 0)
            bodies(dve, body)

        @block.scalar
        def _(act):
            def body(i, k):
                b, slot = 2 * i + k, k % 2
                for hg, t, live in steps(i, k):
                    empties(act, "A", i, k, hg, live, t, 0)
                    if live(t):
                        act.wait_ge(maxed, t + 1)
                        after(act, turned, t - 1)
                        if hg == 0:
                            after(act, normed, b - 1)
                        values = biased[:, hg % 2, :] if cfg.bias else of(S, hg)
                        for g in range(4):
                            h = 4 * hg + g
                            ins = nc.scalar.activation(probs[:, hg % 2, g * P:(g + 1) * P],
                                                       values[:, g * P:(g + 1) * P], ACT.Exp,
                                                       bias=neg_max[:, hg % 2, g:g + 1],
                                                       accum_out=row_sum[:, slot, h:h + 1])
                        ins.then_inc(exped, 1)
                    empties(act, "A", i, k, hg, live, t, 1, 2)

            for n, (name, _, _) in enumerate(cfg.proj):
                if "A" in cfg.reader[name]:
                    take_projected(act, "A", n, 0, 0)
            bodies(act, body)

        @block.gpsimd
        def _(pool):
            def stage(b, slot):
                if cfg.q_scale is None:
                    nc.gpsimd.tensor_copy(src[:, slot, :], cfg.kvT[:, b, :]).then_inc(src_ready, 1)
                else:
                    nc.gpsimd.tensor_copy(k_sb[:, slot, :], cfg.kvT[:, b, :]).then_inc(k_copied, 1)
                    pool.wait_ge(k_copied, b + 1)
                    nc.gpsimd.tensor_tensor(q_sb[:, slot, :], k_sb[:, slot, :], cfg.q_scale.broadcast_to([P, P]), ALU.mult)\
                      .then_inc(src_ready, 1)

            def body(i, k):
                b, slot = 2 * i + k, k % 2
                for hg, t, live in steps(i, k):
                    if narrow and live(t):
                        if hg == 0 and n_proj:
                            wait_read(pool, p_free, n_proj, b + 1, 0)
                        after(pool, scored, t - 1)
                        nc.gpsimd.tensor_tensor(heads4(k_one[:, hg % 2, :]),
                                                k_sb[:, slot, :].unsqueeze(1).broadcast_to([P, 4, P]),
                                                along(G.c["heads"][:, 4 * hg:4 * hg + 4], [P, 4, P]), ALU.mult)\
                          .then_inc(k_ready, 1)
                    if hg == 0 and live(t + HG):
                        if cfg.q_scale is not None:
                            after(pool, scored, HG * b)
                        else:
                            after(pool, p_made, n_proj * b)
                        stage(b + 1, 1 - slot)

            stage(0, 0)
            bodies(pool, body)


def l0_attn(nc, G):
    layernorm(nc, G, "l0_attn", "l0_attn")
    w = G.w["l0_attn"]
    attention(nc, G, Heads(
        tag="l0_attn", dv=8, narrow=True, v_cols=P, kvT=G.xnT, proj=[("qk", 0, 2), ("v", 2, 2)], end=[("t0", 3, 0), ("p", 3, 2)],
        reader=dict(qk="A", v="A", t0="A", p="V"), w=dict(q=w["wq"], k=w["wk"], v=w["wv"], o=w["wo"]), scale=8 ** -0.5,
        mask=G.mask_qk_bf[:].unsqueeze(1).broadcast_to([P, 4, P]), on_keys=G.c["decay"]))


def l1_attn(nc, G):
    w = G.w["l1_attn"]
    with Scope(nc, G, "l1_attn_in") as s:
        q_scale = s.sb("q_scale", [P, 1])
        own = s.sem("own")

        def prepare(dve):
            nc.vector.scalar_tensor_tensor(q_scale[:], w["rot"], 8 ** -0.5, w["ent"], ALU.mult, ALU.mult).then_inc(own, 1)

        layernorm(nc, G, "l1_attn", "l1_attn", also=prepare)
        attention(nc, G, Heads(tag="l1_attn", dv=8, narrow=True, v_cols=0, kvT=G.xnT, proj=[], end=[], reader={}, w={},
                               q_scale=q_scale[:]))


def l1_xattn(nc, G):
    w = G.w["l1_xattn"]
    with Scope(nc, G, "l1_xattn_in") as s:
        cnT = s.sb("cnT", [P, NB, P])
        context = G.ctx1[:].rearrange("p b (h d) -> p b h d", h=8)
        layernorm(nc, G, "l1_xattn", "l1_xattn")
        layernorm(nc, G, "l1_xattn_x", None, src=lambda b: G.xn[:, b, :], gT=w["ln_g"], bT=w["ln_b"])
        layernorm(nc, G, "l1_xattn_c", None, src=lambda b: context[:, b, :, 0:16], outT=cnT,
                  gT=w["cln_g"], bT=w["cln_b"])
        attention(nc, G, Heads(
            tag="l1_xattn", dv=64, narrow=False, q_cols=1024, v_cols=64, kvT=cnT,
            proj=[("q0", 0, 0), ("q1", 0, 2), ("kv", 2, 2)], end=[("t0", 3, 0), ("t1", 3, 1), ("p", 3, 2)],
            reader=dict(q0="A", q1="A", kv="V", t0="A", t1="V", p="V"),
            w=dict(q=w["wq"], k=w["wkk"], v=w["wv"], o=w["wo"]), scale=64 ** -0.5))
    swiglu(nc, G, w)


def swiglu(nc, G, w):
    CH = 4
    with Scope(nc, G, "swiglu") as s:
        gate = s.sb("gate", [P, 2, QT])
        hidden = s.sb("hidden", [P, CH, QT])
        made, gated, multiplied, out_made, added = (s.sem(n) for n in ("made", "gated", "multiplied", "out_made", "added"))
        block = s.block()

        @block.tensor
        def _(pe):
            with pe.Fori(0, NQ) as q:
                tokens = G.xnT[:, bass.ds(q * QUAD, QUAD), :]
                for c in range(CH):
                    if c < 2:
                        pe.wait_ge(multiplied, CH * q)
                    else:
                        pe.wait_ge(multiplied, CH * q + c - 1)
                    nc.tensor.matmul(G.ps[:, 2 * (c % 2), :], w["wff1"][:, (CH + c) * P:(CH + c + 1) * P], tokens,
                                     start=True, stop=True)
                    nc.tensor.matmul(G.ps[:, 2 * (c % 2) + 1, :], w["wff1"][:, c * P:(c + 1) * P], tokens,
                                     start=True, stop=True).then_inc(made, 1)
                pe.wait_ge(multiplied, CH * (q + 1))
                pe.wait_ge(added, q)
                for j in range(QUAD):
                    for c in range(CH):
                        mm = nc.tensor.matmul(G.ps[:, 4, j * P:(j + 1) * P], hidden[:, c, j * P:(j + 1) * P],
                                              w["wff2"][:, c * P:(c + 1) * P], start=c == 0, stop=c == CH - 1)
                mm.then_inc(out_made, 1)

        @block.scalar
        def _(act):
            with act.Fori(0, NQ) as q:
                for c in range(CH):
                    act.wait_ge(made, CH * q + c + 1)
                    if c < 2:
                        act.wait_ge(multiplied, CH * q)
                    else:
                        act.wait_ge(multiplied, CH * q + c - 1)
                    nc.scalar.activation(gate[:, c % 2, :], G.ps[:, 2 * (c % 2), :], ACT.Silu).then_inc(gated, 1)

        @block.vector
        def _(dve):
            with dve.Fori(0, NQ) as q:
                for c in range(CH):
                    dve.wait_ge(gated, CH * q + c + 1)
                    dve.wait_ge(out_made, q)
                    nc.vector.tensor_tensor(hidden[:, c, :], gate[:, c % 2, :], G.ps[:, 2 * (c % 2) + 1, :],
                                            ALU.mult).then_inc(multiplied, 1)
                dve.wait_ge(out_made, q + 1)
                x = G.x[:, bass.ds(q * QUAD, QUAD), :]
                nc.vector.tensor_tensor(x, x, heads4(G.ps[:, 4, :]), ALU.add).then_inc(added, 1)


def l1_ffn(nc, G):
    w = G.w["l1_ffn"]
    K = 32
    layernorm(nc, G, "l1_ffn", "l1_ffn")
    with Scope(nc, G, "l1_ffn") as s:
        moved = s.sb("moved", [K, NB, D])
        odd = s.sb("odd", [K, 2, D])
        even1 = s.sb("even1", [K, 2, 512])
        even2 = s.sb("even2", [K, 2, 512])
        w1 = s.sb("w1", [P, 2, 512])
        w2 = s.sb("w2", [P, 2, 512])
        hT = s.sb("hT", [P, 2, 512])
        zeroed, shifted, staged, low1, low2, w1_set, w2_set, h_made, gelued, out_made, added = (
            s.sem(n) for n in ("zeroed", "shifted", "staged", "low1", "low2", "w1_set", "w2_set", "h_made", "gelued",
                               "out_made", "added"))
        block = s.block()

        @block.sync
        def _(sp):
            sp.wait_ge(zeroed, 1)
            sp.dma_start(moved[1:K, :, :], G.xn[0:K - 1, :, :]).then_inc(shifted, 16)

        @block.gpsimd
        def _(pool):
            nc.gpsimd.memset(moved[:], 0.0).then_inc(zeroed, 1)
            pool.wait_ge(shifted, 16)

            def body(i, k):
                b, slot = 2 * i + k, k % 2
                if whole(b) and b >= NB:
                    return
                after(pool, low2, b - 1)
                nc.gpsimd.tensor_copy(odd[:, slot, :], G.xn[0:K, b, :])
                nc.gpsimd.tensor_tensor(even1[:, slot, :].rearrange("p (i a) -> p i a", i=4),
                                        moved[:, b, :].unsqueeze(1).broadcast_to([K, 4, D]),
                                        along(G.c["pairs"][0:K, 0:4], [K, 4, D]), ALU.mult)
                nc.gpsimd.tensor_tensor(
                    even2[:, slot, :].rearrange("k (r i p) -> k r i p", r=4, i=4),
                    moved[:, b, :].rearrange("k (p r) -> k r p", r=4).unsqueeze(2).broadcast_to([K, 4, 4, 32]),
                    along(G.c["pairs"][0:K, 4:8], [K, 4, 32]).unsqueeze(1).broadcast_to([K, 4, 4, 32]),
                    ALU.mult).then_inc(staged, 1)

            bodies(pool, body)

        @block.tensor
        def _(pe):
            def body(i, k):
                b, slot = 2 * i + k, k % 2
                now, before = not whole(b) or b < NB, not whole(b) or b > 0
                if now:
                    pe.wait_ge(staged, b + 1)
                    after(pe, w1_set, b)
                    nc.tensor.matmul(G.ps[:, 0, :], odd[:, slot, :], even1[:, slot, :], start=True, stop=True)                      .then_inc(low1, 1)
                    after(pe, w2_set, b)
                    nc.tensor.matmul(G.ps[:, 1, :], odd[:, slot, :], even2[:, slot, :], start=True, stop=True)                      .then_inc(low2, 1)
                if before:
                    pe.wait_ge(gelued, b)
                    after(pe, added, b - 1)
                    for c in range(4):
                        nc.tensor.matmul(G.ps[:, 4, 0:P], hT[:, 1 - slot, c * P:(c + 1) * P],
                                         w2[:, 1 - slot, c * P:(c + 1) * P], start=c == 0, stop=False)
                    nc.tensor.matmul(G.ps[:, 4, 0:P], G.c["ones_row"], w["b2"], start=False, stop=True).then_inc(out_made, 1)
                if now:
                    pe.wait_ge(w1_set, b + 1)
                    after(pe, gelued, b - 1)
                    for c in range(4):
                        mm = nc.tensor.matmul(G.ps[:, 2 + slot, c * P:(c + 1) * P], w1[:, slot, c * P:(c + 1) * P],
                                              G.xnT[:, b, :], start=True, stop=True)
                    mm.then_inc(h_made, 1)

            bodies(pe, body)

        @block.vector
        def _(dve):
            def body(i, k):
                b, slot = 2 * i + k, k % 2
                now, before = not whole(b) or b < NB, not whole(b) or b > 0
                if now:
                    dve.wait_ge(low1, b + 1)
                    after(dve, h_made, b - 1)
                    nc.vector.scalar_tensor_tensor(w1[:, slot, :], G.ps[:, 0, :], w["scale"], w["w1"], ALU.mult,
                                                   ALU.add).then_inc(w1_set, 1)
                    dve.wait_ge(low2, b + 1)
                    after(dve, out_made, b - 1)
                    nc.vector.scalar_tensor_tensor(w2[:, slot, :], G.ps[:, 1, :], w["scale"], w["w2"], ALU.mult,
                                                   ALU.add).then_inc(w2_set, 1)
                if before:
                    dve.wait_ge(out_made, b)
                    nc.vector.tensor_tensor(G.x[:, b - 1, :], G.x[:, b - 1, :], G.ps[:, 4, 0:P], ALU.add)                      .then_inc(added, 1)

            bodies(dve, body)

        @block.scalar
        def _(act):
            def body(i, k):
                b, slot = 2 * i + k, k % 2
                if whole(b) and b >= NB:
                    return
                act.wait_ge(h_made, b + 1)
                after(act, out_made, b - 1)
                for c in range(4):
                    ins = nc.scalar.activation(hT[:, slot, c * P:(c + 1) * P], G.ps[:, 2 + slot, c * P:(c + 1) * P],
                                               ACT.Gelu, bias=w["b1"][:, c:c + 1])
                ins.then_inc(gelued, 1)

            bodies(act, body)


def l2_xattn(nc, G):
    w = G.w["l2_xattn"]
    with Scope(nc, G, "l2_xattn_in") as s:
        bias = s.sb("bias", [P, 16, P])
        own = s.sem("own")

        def prepare(dve):
            for h in range(16):
                nc.vector.tensor_scalar(bias[:, h, :], w["bias"], 2.0 ** -(h + 1), None, ALU.mult).then_inc(own, 1)

        layernorm(nc, G, "l2_xattn", "l2_xattn", also=prepare)
        attention(nc, G, Heads(
            tag="l2_xattn", dv=64, narrow=False, q_cols=1024, k_cols=1024, v_cols=1024, kvT=G.ctxT,
            proj=[("q0", 0, 0), ("q1", 0, 2), ("k0", 1, 0), ("k1", 1, 2), ("v0", 2, 0), ("v1", 2, 2)],
            end=[("t0", 3, 0), ("t1", 3, 1), ("p", 3, 2)],
            reader=dict(q0="A", q1="A", k0="V", k1="V", v0="A", v1="A", t0="A", t1="A", p="V"),
            w=dict(q=w["wq"], k=w["wk"], v=w["wv"], o=w["wo"]), scale=64 ** -0.5, b_out=w["b_out"],
            bias=lambda hg: bias[:, 4 * hg:4 * hg + 4, :].rearrange("p h k -> p (h k)")))


def top_two(nc, dve, own, G, logits, top8, work, gates, n):
    link = Link(dve, own)
    for b in range(NB):
        link.note(nc.vector.max(top8[:, b, :], logits[:, b, :]))
    link.catch()
    second = along(top8[:, :, 1], [P, NB, n])
    same, rank, more, keep = (work[:, j, :, :] for j in range(4))
    link.note(nc.vector.memset(keep, 1.0))
    link.catch()
    link.note(nc.vector.memset(keep[:, :, 0:1], 0.0))
    link.note(nc.vector.tensor_tensor(same, logits, second, ALU.is_equal))
    link.note(nc.vector.tensor_tensor(more, logits, second, ALU.is_gt))
    link.catch()
    flat = lambda a: a.rearrange("p b e -> p (b e)")
    link.note(nc.vector.tensor_tensor_scan(flat(rank), flat(keep), flat(same), 0.0, ALU.mult, ALU.add))
    count = top8[:, :, 2]
    link.note(nc.vector.tensor_reduce(count, more, AX.X, ALU.add))
    link.catch()
    link(nc.vector.tensor_tensor(rank, rank, along(count, [P, NB, n]), ALU.add))
    link(nc.vector.scalar_tensor_tensor(flat(rank), flat(rank), 2.0, flat(same), ALU.is_le, ALU.mult))
    link(nc.vector.tensor_tensor(gates, rank, more, ALU.add))
    return link


def l0_moe(nc, G):
    w = G.w["l0_moe"]
    E, CH = 8, 4
    layernorm(nc, G, "l0_moe", "l0_moe")
    with Scope(nc, G, "l0_moe") as s:
        logits = s.sb("logits", [P, NB, E])
        top8 = s.sb("top8", [P, NB, 8])
        work = s.sb("work", [P, 4, NB, E])
        weight = s.sb("weight", [P, NB, E])
        gates = s.sb("gates", [P, NB, E])
        total = s.sb("total", [P, NB])
        gatesT = s.sb("gatesT", [E, NB, P])
        gatesT_q = s.sb("gatesT_q", [E, 2, QT])
        hidden = s.sb("hidden", [P, 2, QT])
        gated = s.sb("gated", [P, 2, CH, QT])
        (scored, own, shifted, exped, gates_set, turned, gatesT_set, staged, made, relued, multiplied, out_made,
         added) = (s.sem(n) for n in ("scored", "own", "shifted", "exped", "gates_set", "turned", "gatesT_set",
                                      "staged", "made", "relued", "multiplied", "out_made", "added"))
        block = s.block()

        @block.tensor
        def _(pe):
            for b in range(NB):
                mm = nc.tensor.matmul(G.ps[:, 0, b * E:(b + 1) * E], G.xnT[:, b, :], w["wg"], start=True, stop=True)
            mm.then_inc(scored, 1)
            pe.wait_ge(gates_set, 1)
            for b in range(NB):
                mm = nc.tensor.transpose(G.ps[0:E, 4 + b // 4, (b % 4) * P:(b % 4 + 1) * P], gates[:, b, :], G.c["ident"])
            mm.then_inc(turned, 1)
            pe.wait_ge(gatesT_set, 1)
            with pe.Fori(0, NQ // 2) as i:
                for k in range(2):
                    q = 2 * i + k
                    tokens = G.xnT[:, bass.ds(q * QUAD, QUAD), :]
                    for c in range(CH):
                        if k == 0 and c < 2:
                            pe.wait_ge(multiplied, CH * 2 * i)
                        else:
                            pe.wait_ge(multiplied, CH * q + c - 1)
                        nc.tensor.matmul(G.ps[:, 2 * (c % 2), :], w["wd"][:, c * P:(c + 1) * P], tokens, start=True, stop=True)
                        nc.tensor.matmul(G.ps[:, 2 * (c % 2) + 1, :], G.c["sel_e"][:, c * P:(c + 1) * P],
                                         gatesT[:, bass.ds(q * QUAD, QUAD), :], start=True, stop=True).then_inc(made, 1)
                    pe.wait_ge(multiplied, CH * (q + 1))
                    pe.wait_ge(staged, q + 1)
                    pe.wait_ge(added, q)
                    for j in range(QUAD):
                        tok = slice(j * P, (j + 1) * P)
                        for c in range(CH):
                            nc.tensor.matmul(G.ps[:, 4, tok], gated[:, k, c, tok], w["wu"][:, c * P:(c + 1) * P],
                                             start=c == 0, stop=False)
                        mm = nc.tensor.matmul(G.ps[:, 4, tok], gatesT_q[:, k, tok], w["bu"], start=False, stop=True)
                    mm.then_inc(out_made, 1)

        @block.scalar
        def _(act):
            act.wait_ge(shifted, 1)
            nc.scalar.activation(weight[:], work[:, 0, :, :], ACT.Exp).then_inc(exped, 1)
            act.wait_ge(turned, 1)
            nc.scalar.copy(gatesT[:].rearrange("p b t -> p (b t)"),
                           G.ps[0:E, 4:8, :].rearrange("p b t -> p (b t)")).then_inc(gatesT_set, 1)
            with act.Fori(0, NQ // 2) as i:
                for k in range(2):
                    q = 2 * i + k
                    for c in range(CH):
                        act.wait_ge(made, CH * q + c + 1)
                        for_slot = CH * 2 * i if k == 0 and c < 2 else CH * q + c - 1
                        act.wait_ge(multiplied, for_slot)
                        nc.scalar.activation(hidden[:, c % 2, :], G.ps[:, 2 * (c % 2), :], ACT.Relu,
                                             bias=w["bd"][:, c:c + 1]).then_inc(relued, 1)

        @block.vector
        def _(dve):
            dve.wait_ge(scored, 1)
            link0 = Link(dve, own)
            link0(nc.vector.tensor_copy(logits[:].rearrange("p b e -> p (b e)"), G.ps[:, 0, 0:NB * E]))
            link = top_two(nc, dve, s.sem("own_top"), G, logits[:], top8[:], work[:], gates[:], E)
            nc.vector.tensor_tensor(work[:, 0, :, :], logits[:], along(top8[:, :, 0], [P, NB, E]), ALU.subtract)              .then_inc(shifted, 1)
            dve.wait_ge(exped, 1)
            link(nc.vector.tensor_tensor(gates[:], gates[:], weight[:], ALU.mult))
            link(nc.vector.tensor_reduce(total[:], gates[:], AX.X, ALU.add))
            link(nc.vector.reciprocal(total[:], total[:]))
            link(nc.vector.tensor_scalar(total[:], total[:], 0.5, None, ALU.mult))
            nc.vector.tensor_tensor(gates[:], gates[:], along(total[:], [P, NB, E]), ALU.mult).then_inc(gates_set, 1)
            with dve.Fori(0, NQ // 2) as i:
                for k in range(2):
                    q = 2 * i + k
                    for c in range(CH):
                        dve.wait_ge(relued, CH * q + c + 1)
                        dve.wait_ge(out_made, 2 * i)
                        nc.vector.tensor_tensor(gated[:, k, c, :], hidden[:, c % 2, :], G.ps[:, 2 * (c % 2) + 1, :],
                                                ALU.mult).then_inc(multiplied, 1)
                    dve.wait_ge(out_made, q + 1)
                    x = G.x[:, bass.ds(q * QUAD, QUAD), :]
                    nc.vector.tensor_tensor(x, x, heads4(G.ps[:, 4, :]), ALU.add).then_inc(added, 1)

        @block.gpsimd
        def _(pool):
            pool.wait_ge(gatesT_set, 1)
            with pool.Fori(0, NQ // 2) as i:
                for k in range(2):
                    q = 2 * i + k
                    pool.wait_ge(out_made, 2 * i)
                    nc.gpsimd.tensor_copy(gatesT_q[:, k, :].rearrange("p (b t) -> p b t", b=QUAD),
                                          gatesT[:, bass.ds(q * QUAD, QUAD), :]).then_inc(staged, 1)


def l0_mlstm(nc, G):
    w = G.w["l0_mlstm"]
    H, DH, CAP = 8, 16, 15.0
    W = DH + 1
    layernorm(nc, G, "l0_mlstm", "l0_mlstm", more=("ctxT", "ctx1"))
    with Scope(nc, G, "l0_mlstm") as s:
        bias15 = s.sb("bias15", [P, 2])
        wkv = s.sb("wkv", [P, 2 * H])
        gain = s.sb("gain", [P, D])
        zeros = s.sb("zeros", [P, P])
        gates = s.sb("gates", [P, 2, NB, H])
        gate_i, gate_f = s.sb("gate_i", [P, P]), s.sb("gate_f", [P, P])
        cs = s.sb("cs", [P, P])
        a_row = s.sb("a_row", [P, P])
        neg_m = s.sb("neg_m", [P, P])
        floor_row = s.sb("floor_row", [P, P])
        cols = s.sb("cols", [P, 3, NB, H])
        a_col, m_col, floor_col = (cols[:, n, :, :] for n in range(3))
        k_one, q_one = s.sb("k_one", [P, 2, P]), s.sb("q_one", [P, 2, P])
        m_one = s.sb("m_one", [P, 2, H])
        q_head = s.sb("q_head", [P, 2, 2, 512])
        decay = s.sb("decay", [P, 2, 512])
        weights = s.sb("weights", [P, 2, 512])
        den, ms, rrms = (s.sb(n, [P, H]) for n in ("den", "ms", "rrms"))
        neg_half = s.sb("neg_half", [P, H])
        hid, square = s.sb("hid", [P, H, DH]), s.sb("square", [P, H, DH])
        (wkv_set, gates_made, gates_copied, gates_turned, gates_set, logs_set, own, rows_set, floor_set, cols_turned,
         cols_set, staged, m_staged, q_ready, e_made, s_made, exped, multiplied, summed, o_read, ms_set, rrms_set,
         added, exponent) = (s.sem(n) for n in (
             "wkv_set", "gates_made", "gates_copied", "gates_turned", "gates_set", "logs_set", "own", "rows_set",
             "floor_set", "cols_turned", "cols_set", "staged", "m_staged", "q_ready", "e_made", "s_made", "exped",
             "multiplied", "summed", "o_read", "ms_set", "rrms_set", "added", "exponent"))
        block = s.block()

        @block.tensor
        def _(pe):
            pe.wait_ge(wkv_set, 1)
            for b in range(NB):
                out = G.ps[:, 6, b * 2 * H:(b + 1) * 2 * H]
                nc.tensor.matmul(out, G.xnT[:, b, :], w["wg"][:, 0:2 * H], start=True, stop=False)
                mm = nc.tensor.matmul(out, G.ctxT[:, b, :], wkv[:], start=False, stop=True)
            mm.then_inc(gates_made, 1)
            pe.wait_ge(gates_copied, 1)
            for n in range(2):
                mm = nc.tensor.transpose(G.ps[:, 7, n * P:(n + 1) * P], gates[:, n, :, :].rearrange("p b h -> p (b h)"),
                                         G.c["ident"])
            mm.then_inc(gates_turned, 1)
            pe.wait_ge(rows_set, 1)
            pe.wait_ge(floor_set, 1)
            for n, row in enumerate((a_row, neg_m, floor_row)):
                mm = nc.tensor.transpose(G.ps[:, 6, n * P:(n + 1) * P], row[:], G.c["ident"])
            mm.then_inc(cols_turned, 1)

            def times_v(b, step, slot):
                t = 2 * b + step
                pe.wait_ge(multiplied, t + 1)
                if step == 0:
                    after(pe, o_read, b - 1)
                for g in range(4):
                    h = 4 * step + g
                    mm = nc.tensor.matmul(G.ps[:, 4 + slot, h * W:(h + 1) * W], weights[:, step, g * P:(g + 1) * P],
                                          G.ctx1[:, b, h * W:(h + 1) * W], start=True, stop=True)
                mm.then_inc(summed, 1)

            def body(i, k):
                b, slot = 2 * i + k, k % 2
                now, before = not whole(b) or b < NB, not whole(b) or b > 0
                for step in range(2):
                    t = 2 * b + step
                    if now:
                        if step == 0:
                            pe.wait_ge(m_staged, b + 1)
                            pe.wait_ge(staged, b + 1)
                        after(pe, exped, t - 1)
                        nc.tensor.matmul(G.ps[:, step, :], G.ident_bf[:],
                                         G.mask_kq_bf[:].unsqueeze(1).broadcast_to([P, 4, P]),
                                         start=True, stop=False, skip_group_check=True)
                        for g in range(4):
                            h = 4 * step + g
                            mm = nc.tensor.matmul(G.ps[:, step, g * P:(g + 1) * P],
                                                  m_one[:, slot, h:h + 1].broadcast_to([P, P]), G.c["ident"],
                                                  start=False, stop=True, skip_group_check=True)
                        mm.then_inc(e_made, 1)
                        pe.wait_ge(q_ready, t + 1)
                        after(pe, multiplied, t - 1)
                        nc.tensor.matmul(G.ps[:, 2 + step, :], k_one[:, slot, :], q_head[:, slot, step, :], start=True, stop=True)\
                          .then_inc(s_made, 1)
                    if step == 0 and before:
                        times_v(b - 1, 1, 1 - slot)
                    if step == 1 and now:
                        times_v(b, 0, slot)

            bodies(pe, body)

        @block.scalar
        def _(act):
            act.wait_ge(gates_made, 1)
            nc.scalar.copy(gates[:].rearrange("p g b h -> p b g h"),
                           G.ps[:, 6, 0:2 * H * NB].rearrange("p (b g h) -> p b g h", b=NB, g=2)).then_inc(gates_copied, 1)
            act.wait_ge(gates_turned, 1)
            act.wait_ge(wkv_set, 1)
            for n, gate in enumerate((gate_f, gate_i)):
                nc.scalar.activation(gate[:], G.ps[:, 7, (1 - n) * P:(2 - n) * P], ACT.Tanh, bias=bias15[:, 1 - n:2 - n],
                                     scale=1.0 / CAP).then_inc(gates_set, 1)
            act.wait_ge(gates_set, 1)
            nc.scalar.activation(gate_f[:], gate_f[:], ACT.Exp, scale=-CAP).then_inc(gates_set, 1)
            act.wait_ge(gates_set, 3)
            nc.scalar.activation(gate_f[:], gate_f[:], ACT.Ln, bias=1.0).then_inc(logs_set, 1)
            act.wait_ge(rows_set, 1)
            nc.scalar.activation(floor_row[:], floor_row[:], ACT.Exp).then_inc(floor_set, 1)
            act.wait_ge(cols_turned, 1)
            nc.scalar.copy(cols[:].rearrange("p n b h -> p (n b h)"), G.ps[:, 6, 0:3 * NB * H]).then_inc(cols_set, 1)
            act.wait_ge(cols_set, 1)

            def stage(b, slot):
                nc.scalar.copy(k_one[:, slot, :], G.ctxT[:, b, :])
                nc.scalar.copy(q_one[:, slot, :], G.xnT[:, b, :]).then_inc(staged, 1)

            def body(i, k):
                b, slot = 2 * i + k, k % 2
                if whole(b) and b >= NB:
                    return
                for step in range(2):
                    t = 2 * b + step
                    act.wait_ge(e_made, t + 1)
                    after(act, multiplied, t - 1)
                    for g in range(4):
                        h = 4 * step + g
                        ins = nc.scalar.activation(decay[:, step, g * P:(g + 1) * P], G.ps[:, step, g * P:(g + 1) * P],
                                                   ACT.Exp, bias=a_col[:, b, h:h + 1])
                    ins.then_inc(exped, 1)
                    if step == 0 and (not whole(b) or b + 1 < NB):
                        after(act, s_made, 2 * b)
                        after(act, q_ready, 2 * b)
                        stage(b + 1, 1 - slot)

            stage(0, 0)
            bodies(act, body)

        @block.vector
        def _(dve):
            nc.vector.memset(zeros[:], 0.0)
            nc.vector.tensor_scalar(bias15[:], w["bias"], 1.0 / CAP, None, ALU.mult)
            nc.vector.tensor_scalar(gain[:], w["gain"], 1.0, None, ALU.add)
            nc.vector.tensor_tensor(wkv[:], w["wg"][:, 2 * H:4 * H], w["wg"][:, 4 * H:6 * H], ALU.add).then_inc(wkv_set, 1)
            dve.wait_ge(wkv_set, 1)
            dve.wait_ge(logs_set, 1)
            dve.wait_ge(gates_set, 2)
            link = Link(dve, own)
            link(nc.vector.tensor_tensor_scan(cs[:], G.ones[:, 0:P], gate_f[:], 0.0, ALU.mult, ALU.add))
            link(nc.vector.scalar_tensor_tensor(a_row[:], gate_i[:], CAP, cs[:], ALU.mult, ALU.add))
            link(nc.vector.tensor_tensor_scan(neg_m[:], zeros[:], a_row[:], NEG, ALU.add, ALU.max))
            link(nc.vector.tensor_tensor(floor_row[:], cs[:], neg_m[:], ALU.subtract))
            nc.vector.tensor_scalar(neg_m[:], neg_m[:], -1.0, None, ALU.mult).then_inc(rows_set, 1)
            dve.wait_ge(cols_set, 1)
            base, PER = link.n, 9

            def normalize(b, slot):
                link = Link(dve, own, base + PER * b)
                sums = G.ps[:, 4 + slot, 0:H * W].rearrange("p (h w) -> p h w", w=W)
                row_sum = sums[:, :, DH]
                link(nc.vector.tensor_scalar(ms[:], row_sum, -1.0, None, ALU.mult))
                link(nc.vector.tensor_tensor(den[:], row_sum, ms[:], ALU.max))
                link(nc.vector.tensor_tensor(den[:], den[:], floor_col[:, b, :], ALU.max))
                link(nc.vector.tensor_scalar(den[:], den[:], 5e-5, None, ALU.add))
                link(nc.vector.reciprocal(den[:], den[:]))
                nc.vector.tensor_tensor(hid[:], sums[:, :, 0:DH], along(den[:], [P, H, DH]), ALU.mult).then_inc(o_read, 1)
                dve.wait_ge(o_read, b + 1)
                link(nc.vector.tensor_tensor(square[:], hid[:], hid[:], ALU.mult))
                link(nc.vector.tensor_reduce(ms[:], square[:], AX.X, ALU.add))
                nc.vector.tensor_scalar(ms[:], ms[:], 1.0 / DH, 1e-6, ALU.mult, ALU.add).then_inc(ms_set, 1)

            def add(b):
                link = Link(dve, own, base + PER * b + 7)
                dve.wait_ge(rrms_set, b + 1)
                flat = hid[:].rearrange("p h d -> p (h d)")
                link(nc.vector.tensor_tensor(hid[:], hid[:], along(rrms[:], [P, H, DH]), ALU.mult))
                link(nc.vector.tensor_tensor(flat, flat, gain[:], ALU.mult))
                nc.vector.tensor_tensor(G.x[:, b, :], G.x[:, b, :], flat, ALU.add).then_inc(added, 1)
                dve.wait_ge(added, b + 1)

            def body(i, k):
                b, slot = 2 * i + k, k % 2
                now, before = not whole(b) or b < NB, not whole(b) or b > 0
                for step in range(2):
                    t = 2 * b + step
                    if now:
                        dve.wait_ge(exped, t + 1)
                        dve.wait_ge(s_made, t + 1)
                        after(dve, summed, t - 1)
                        nc.vector.tensor_tensor(weights[:, step, :], G.ps[:, 2 + step, :], decay[:, step, :], ALU.mult)\
                          .then_inc(multiplied, 1)
                    if before and step == 0:
                        if not whole(b) or b > 1:
                            add(b - 2)
                        dve.wait_ge(summed, 2 * b)
                        normalize(b - 1, 1 - slot)

            body(0, 0)
            body(0, 1)
            with dve.Fori(1, NB // 2) as i:
                body(i, 0)
                body(i, 1)
            body(0, NB)
            add(NB - 1)

        @block.gpsimd
        def _(pool):
            nc.gpsimd.memset(neg_half[:], -0.5).then_inc(exponent, 1)
            pool.wait_ge(exponent, 1)
            pool.wait_ge(cols_set, 1)

            def stage(b, slot):
                after(pool, s_made, 2 * (b - 1))
                nc.gpsimd.tensor_copy(m_one[:, slot, :], m_col[:, b, :]).then_inc(m_staged, 1)
                pool.wait_ge(staged, b + 1)
                for step in range(2):
                    nc.gpsimd.tensor_tensor(heads4(q_head[:, slot, step, :]),
                                            q_one[:, slot, :].unsqueeze(1).broadcast_to([P, 4, P]),
                                            along(G.c["heads16"][:, 4 * step:4 * step + 4], [P, 4, P]), ALU.mult)\
                      .then_inc(q_ready, 1)

            def body(i, k):
                b, slot = 2 * i + k, k % 2
                if not whole(b) or b + 1 < NB:
                    stage(b + 1, 1 - slot)
                if not whole(b) or b > 0:
                    pool.wait_ge(ms_set, b)
                    after(pool, added, b - 1)
                    nc.gpsimd.tensor_tensor(rrms[:], ms[:], neg_half[:], ALU.pow).then_inc(rrms_set, 1)

            stage(0, 0)
            bodies(pool, body)


def l2_mamba(nc, G):
    w = G.w["l2_mamba"]
    R, NS, PAD = 64, 16, 3
    layernorm(nc, G, "l2_mamba", "l2_mamba", fetch="l3_moe")
    with Scope(nc, G, "l2_mamba") as s:
        A = s.sb("A", [P, 2, NS])
        xp = s.sb("xp", [P, 2, QUAD, PAD + P])
        conv = s.sb("conv", [P, 2, QUAD, P])
        xc = s.sb("xc", [P, 2, QUAD, P])
        z = s.sb("z", [P, 2, QUAD, P])
        xd = s.sb("xd", [P, QT])
        rest = s.sb("rest", [2 * NS, QT])
        part = s.sb("part", [2 * NS, QT], BF16)
        bc3 = s.sb("bc3", [3 * 2 * NS, QT], BF16)
        dt = s.sb("dt", [P, 2, QUAD, P])
        dtx = s.sb("dtx", [P, 2, QUAD, P])
        dA = s.sb("dA", [P, 2, QUAD, 1 + P])
        dBx = s.sb("dBx", [P, 2, QUAD, 1 + P])
        h = s.sb("h", [P, 2, 2, QUAD, 1 + P])
        c_sb = s.sb("c", [P, 2, QUAD, P])
        hc = s.sb("hc", [P, 2, 2, QT])
        y = s.sb("y", [P, 2, QUAD, P])
        (zeroed, a_set, s1_made, s1_read, own, conv_set, xc_set, dtx_set, bc_split, bc_made, c_copied, dA_set, dBx_set, h_set,
         hc_set, y_summed, y_set, out_made, added) = (s.sem(n) for n in (
             "zeroed", "a_set", "s1_made", "s1_read", "own", "conv_set", "xc_set", "dtx_set", "bc_split", "bc_made", "c_copied",
             "dA_set", "dBx_set", "h_set", "hc_set", "y_summed", "y_set", "out_made", "added"))
        N1 = 7
        M = 2 * NS
        block = s.block()
        bank4 = lambda n: heads4(G.ps[:, n, :])

        @block.tensor
        def _(pe):
            with pe.Fori(0, NQ) as q:
                tokens = G.xnT[:, bass.ds(q * QUAD, QUAD), :]

                def room(p):
                    pe.wait_ge(s1_read, N1 * q + max(p - 1, 0))

                for p in range(4):
                    room(p)
                    nc.tensor.matmul(G.ps[:, 6 + p % 2, :], w["w_in"][:, p * P:(p + 1) * P], tokens, start=True, stop=True)\
                      .then_inc(s1_made, 1)
                room(4)
                pe.wait_ge(xc_set, 2 * (q + 1))
                for half in range(2):
                    mm = nc.tensor.matmul(G.ps[:, 6, :], w["w_x"][:, half * P:(half + 1) * P], xc[:, half, :, :],
                                          start=half == 0, stop=half == 1)
                mm.then_inc(s1_made, 1)
                pe.wait_ge(s1_read, N1 * q + 5)
                for half in range(2):
                    room(5 + half)
                    nc.tensor.matmul(G.ps[:, 7 - half, :], w["w_dt"][:, half * P:(half + 1) * P], xd[:],
                                     start=True, stop=True).then_inc(s1_made, 1)

                def spread(n):
                    pe.wait_ge(dBx_set, M * q + max(2 * (n - 1), 0))
                    pe.wait_ge(c_copied, NS * q + max(n - 1, 0))
                    if n == 0:
                        pe.wait_ge(added, q)
                        pe.wait_ge(bc_split, q + 1)
                    for bank, row in ((n % 2, n), (2 + n % 2, NS + n)):
                        mm = nc.tensor.matmul(G.ps[:, bank, :], G.rows3_bf[:, row:row + 1].broadcast_to([3 * 2 * NS, P]),
                                              bc3[:], start=True, stop=True)
                    mm.then_inc(bc_made, 1)

                def sum_states(n):
                    for half in range(2):
                        m = 2 * n + half
                        pe.wait_ge(hc_set, M * q + m + 1)
                        if n == 0:
                            pe.wait_ge(y_set, 2 * q)
                        nc.tensor.matmul(G.ps[:, 4 + half, :], G.c["ident"], hc[:, n % 2, half, :], start=n == 0,
                                         stop=n == NS - 1).then_inc(y_summed, 1)

                spread(0)
                spread(1)
                for n in range(NS):
                    if n + 2 < NS:
                        spread(n + 2)
                    sum_states(n)
                pe.wait_ge(y_set, 2 * (q + 1))
                for j in range(QUAD):
                    for half in range(2):
                        mm = nc.tensor.matmul(G.ps[:, 0, j * P:(j + 1) * P], y[:, half, j, :],
                                              w["w_out"][:, half * D:(half + 1) * D], start=half == 0, stop=half == 1)
                mm.then_inc(out_made, 1)

        @block.scalar
        def _(act):
            nc.scalar.activation(A[:].rearrange("p a n -> p (a n)"), w["a_log"], ACT.Exp).then_inc(a_set, 1)
            act.wait_ge(zeroed, 1)
            with act.Fori(0, NQ) as q:
                act.wait_ge(conv_set, 2 * q)
                act.wait_ge(y_set, 2 * q)
                for half in range(2):
                    act.wait_ge(s1_made, N1 * q + half + 1)
                    nc.scalar.copy(xp[:, half, :, PAD:], bank4(6 + half)).then_inc(s1_read, 1)
                for half in range(2):
                    act.wait_ge(s1_made, N1 * q + half + 3)
                    nc.scalar.activation(z[:, half, :, :], bank4(6 + half), ACT.Silu).then_inc(s1_read, 1)
                for half in range(2):
                    act.wait_ge(conv_set, 2 * q + half + 1)
                    nc.scalar.activation(xc[:, half, :, :], conv[:, half, :, :], ACT.Silu,
                                         bias=w["conv_b"][:, half:half + 1]).then_inc(xc_set, 1)
                act.wait_ge(bc_made, NS * q)
                act.wait_ge(s1_made, N1 * q + 5)
                nc.scalar.copy(xd[:], G.ps[:, 6, :]).then_inc(s1_read, 1)
                for half in range(2):
                    act.wait_ge(s1_made, N1 * q + 6 + half)
                    nc.scalar.activation(dt[:, half, :, :], bank4(7 - half), ACT.Sigmoid,
                                         bias=w["b_dt"][:, half:half + 1]).then_inc(s1_read, 1)
                for n in range(NS):
                    for half in range(2):
                        m = 2 * n + half
                        act.wait_ge(h_set, M * q + max(m - 1, 0))
                        if n == 0:
                            act.wait_ge(dtx_set, 2 * q + half + 1)
                        nc.scalar.activation(dA[:, half, :, 1:], dt[:, half, :, :], ACT.Exp,
                                             scale=A[:, half, n:n + 1]).then_inc(dA_set, 1)
                    act.wait_ge(bc_made, NS * q + n + 1)
                    act.wait_ge(hc_set, M * q + max(2 * (n - 1), 0))
                    nc.scalar.copy(c_sb[:, n % 2, :, :], bank4(2 + n % 2)).then_inc(c_copied, 1)

        @block.vector
        def _(dve):
            link = Link(dve, own)
            dve.wait_ge(a_set, 1)
            link(nc.vector.tensor_scalar(A[:], A[:], -1.0, None, ALU.mult))
            PER = 2 * (3 + 2) + 5 + 2
            dve.wait_ge(zeroed, 1)
            with dve.Fori(0, NQ) as q:
                link = Link(dve, own, 1 + PER * q)
                for half in range(2):
                    dve.wait_ge(s1_read, N1 * q + half + 1)
                    dve.wait_ge(xc_set, 2 * q)
                    tap = lambda t: w["conv_w"][:, half * 4 + t:half * 4 + t + 1]
                    out = conv[:, half, :, :]
                    link(nc.vector.tensor_scalar(out, xp[:, half, :, 0:P], tap(0), None, ALU.mult))
                    for t in range(1, 4):
                        ins = nc.vector.scalar_tensor_tensor(out, xp[:, half, :, t:t + P], tap(t), out, ALU.mult, ALU.add)
                        if t < 3:
                            link(ins)
                    ins.then_inc(conv_set, 1)
                dve.wait_ge(s1_read, N1 * q + 5)
                rows = lambda n: bc3[2 * NS * n:2 * NS * (n + 1), :]
                link(nc.vector.tensor_copy(rows(0), xd[0:2 * NS, :]))
                link(nc.vector.tensor_tensor(rest[:], xd[0:2 * NS, :], rows(0), ALU.subtract))
                link(nc.vector.tensor_copy(part[:], rest[:]))
                link.note(nc.vector.tensor_copy(rows(1), part[:]))
                link(nc.vector.tensor_tensor(rest[:], rest[:], part[:], ALU.subtract))
                nc.vector.tensor_copy(rows(2), rest[:]).then_inc(bc_split, 1)
                for half in range(2):
                    dve.wait_ge(s1_read, N1 * q + 6 + half)
                    link(nc.vector.tensor_scalar(dt[:, half, :, :], dt[:, half, :, :], 0.1 - 0.001, 0.001, ALU.mult, ALU.add))
                    link(nc.vector.tensor_scalar(dt[:, half, :, :], dt[:, half, :, :], 0.0001, None, ALU.max))
                    nc.vector.tensor_tensor(dtx[:, half, :, :], dt[:, half, :, :], xc[:, half, :, :], ALU.mult)\
                      .then_inc(dtx_set, 1)
                dve.wait_ge(dtx_set, 2 * (q + 1))
                for n in range(NS):
                    dve.wait_ge(bc_made, NS * q + n + 1)
                    for half in range(2):
                        m = 2 * n + half
                        dve.wait_ge(h_set, M * q + max(m - 1, 0))
                        nc.vector.tensor_tensor(dBx[:, half, :, 1:], dtx[:, half, :, :], bank4(n % 2), ALU.mult)\
                          .then_inc(dBx_set, 1)
                    for half in range(2):
                        m = 2 * n + half
                        dve.wait_ge(dBx_set, M * q + m + 1)
                        dve.wait_ge(dA_set, M * q + m + 1)
                        dve.wait_ge(hc_set, M * q + max(m - 3, 0))
                        flat = lambda a: a.rearrange("p b t -> p (b t)")
                        nc.vector.tensor_tensor_scan(flat(h[:, n % 2, half, :, :]), flat(dA[:, half, :, :]),
                                                     flat(dBx[:, half, :, :]), 0.0, ALU.mult, ALU.add)\
                          .then_inc(h_set, 1)
                dve.wait_ge(y_summed, M * (q + 1))
                dve.wait_ge(out_made, q)
                for half in range(2):
                    link(nc.vector.scalar_tensor_tensor(y[:, half, :, :], xc[:, half, :, :], w["d_skip"][:, half:half + 1],
                                                        bank4(4 + half), ALU.mult, ALU.add))
                    nc.vector.tensor_tensor(y[:, half, :, :], y[:, half, :, :], z[:, half, :, :], ALU.mult)\
                      .then_inc(y_set, 1)
                dve.wait_ge(out_made, q + 1)
                x = G.x[:, bass.ds(q * QUAD, QUAD), :]
                nc.vector.tensor_tensor(x, x, bank4(0), ALU.add).then_inc(added, 1)

        @block.gpsimd
        def _(pool):
            nc.gpsimd.memset(xp[:], 0.0)
            nc.gpsimd.memset(dA[:], 0.0)
            nc.gpsimd.memset(dBx[:], 0.0).then_inc(zeroed, 1)
            with pool.Fori(0, NQ) as q:
                for n in range(NS):
                    pool.wait_ge(c_copied, NS * q + n + 1)
                    for half in range(2):
                        m = 2 * n + half
                        pool.wait_ge(h_set, M * q + m + 1)
                        pool.wait_ge(y_summed, M * q + max(m - 3, 0))
                        nc.gpsimd.tensor_tensor(heads4(hc[:, n % 2, half, :]), h[:, n % 2, half, :, 1:],
                                                c_sb[:, n % 2, :, :], ALU.mult).then_inc(hc_set, 1)


FP4 = 16
FP4_OPS = 17


def fp4(nc, link, src, out, work, small):
    n = src.shape[1]
    v = nc.vector
    flat = lambda a: a.rearrange("p n k -> p (n k)")
    scaled, size, count = (w[:, 0:n * FP4] for w in work)
    scale, inverse = (m[:, 0:n] for m in small)
    blocks = lambda a: a.rearrange("p (n k) -> p n k", k=FP4)
    link(v.tensor_reduce(scale, src, AX.X, ALU.max, apply_absolute_value=True))
    link(v.tensor_scalar(scale, scale, 1.0 / 6.0, 1e-12, ALU.mult, ALU.max))
    link(v.reciprocal(inverse, scale))
    link(v.tensor_tensor(blocks(scaled), src, along(inverse, [P, n, FP4]), ALU.mult))
    link(v.scalar_tensor_tensor(size, scaled, -1.0, scaled, ALU.mult, ALU.max))
    link(v.tensor_scalar(count, size, 0.25, None, ALU.is_gt))
    for middle in (0.75, 1.25, 1.75):
        link(v.scalar_tensor_tensor(count, size, middle, count, ALU.is_gt, ALU.add))
    link(v.tensor_scalar(count, count, 0.5, None, ALU.mult))
    for middle in (2.5, 3.5, 5.0, 5.0):
        link(v.scalar_tensor_tensor(count, size, middle, count, ALU.is_gt, ALU.add))
    link(v.tensor_scalar(size, scaled, 0.0, 2.0, ALU.is_ge, ALU.mult))
    link(v.scalar_tensor_tensor(count, size, -1.0, count, ALU.add, ALU.mult))
    link(v.tensor_tensor(out, blocks(count), along(scale, [P, n, FP4]), ALU.mult))


def l2_ffn(nc, G):
    w = G.w["l2_ffn"]
    I = 352
    CH = [(0, 128), (128, 128), (256, 96)]
    layernorm(nc, G, "l2_ffn", "l2_ffn")
    with Scope(nc, G, "l2_ffn") as s:
        wgT = s.sb("wgT", [P, 384])
        wuT = s.sb("wuT", [P, 384])
        wdT = s.sb("wdT", [P, 3, D])
        work = [s.sb(f"work{n}", [P, QUAD * I]) for n in range(3)]
        small = [s.sb(f"small{n}", [P, QUAD * I // FP4]) for n in range(2)]
        xq = s.sb("xq", [P, QUAD, D])
        xqT = s.sb("xqT", [P, QT])
        gate = s.sb("gate", [P, 2, I])
        hid = s.sb("hid", [P, QUAD, I])
        hidT = s.sb("hidT", [P, 2, 3, P])
        (own, own_pe, w_turned, w_copied, x_turned, x_copied, gu_made, gated, h_made, h_turned, h_copied,
         out_made, added) = (s.sem(n) for n in (
             "own", "own_pe", "w_turned", "w_copied", "x_turned", "x_copied", "gu_made", "gated", "h_made",
             "h_turned", "h_copied", "out_made", "added"))
        block = s.block()
        group = G.pack["l2_ffn"]
        blocks = lambda a: a.rearrange("p (n k) -> p n k", k=FP4)

        @block.vector
        def _(dve):
            link = Link(dve, own)
            weights = blocks(group)
            fp4(nc, link, weights, weights, work, small)
            PER = 2 * FP4_OPS

            def round_x(q, link):
                src = G.xn[:, bass.ds(q * QUAD, QUAD), :].rearrange("p b (n k) -> p (b n) k", k=FP4)
                dve.wait_ge(x_turned, q)
                fp4(nc, link, src, blocks(xq[:].rearrange("p b d -> p (b d)")), work, small)

            def body(q, last):
                link = Link(dve, own, FP4_OPS * 2 + PER * q)
                for j in range(QUAD):
                    dve.wait_ge(gated, QUAD * q + j + 1)
                    dve.wait_ge(h_turned, QUAD * q)
                    nc.vector.tensor_tensor(hid[:, j, :], gate[:, j % 2, :], G.ps[:, 2 + 2 * (j % 2), 0:I], ALU.mult)\
                      .then_inc(h_made, 1)
                dve.wait_ge(h_made, QUAD * (q + 1))
                flat = blocks(hid[:].rearrange("p b i -> p (b i)"))
                fp4(nc, link, flat, flat, work, small)
                if not last:
                    round_x(q + 1, link)
                dve.wait_ge(out_made, q + 1)
                x = G.x[:, bass.ds(q * QUAD, QUAD), :]
                nc.vector.tensor_tensor(x, x, heads4(G.ps[:, 6, :]), ALU.add).then_inc(added, 1)

            round_x(0, link)
            with dve.Fori(0, NQ - 1) as q:
                body(q, False)
            body(NQ - 1, True)

        @block.tensor
        def _(pe):
            pe.wait_ge(own, FP4_OPS)
            for n, wt in enumerate((w["wg"], w["wu"])):
                for c, (lo, rows) in enumerate(CH):
                    nc.tensor.transpose(G.ps[:, n, c * P:c * P + rows], wt[0:rows, c * P:(c + 1) * P],
                                        G.c["ident"][0:rows, 0:rows])
            for c, (lo, rows) in enumerate(CH):
                mm = nc.tensor.transpose(G.ps[0:rows, 2, c * P:(c + 1) * P], w["wd"][:, lo:lo + rows], G.c["ident"])
            mm.then_inc(w_turned, 1)
            pe.wait_ge(w_copied, 1)
            FIRST = FP4_OPS * 2
            with pe.Fori(0, NQ) as q:
                pe.wait_ge(own, FIRST + 2 * FP4_OPS * q)
                for j in range(QUAD):
                    mm = nc.tensor.transpose(G.ps[:, 0, j * P:(j + 1) * P], xq[:, j, :], G.c["ident"])
                mm.then_inc(x_turned, 1)
                pe.wait_ge(x_copied, q + 1)
                for j in range(QUAD):
                    pe.wait_ge(h_made, QUAD * q + max(j - 1, 0))
                    nc.tensor.matmul(G.ps[:, 1 + 2 * (j % 2), 0:I], xqT[:, j * P:(j + 1) * P], wgT[:, 0:I],
                                     start=True, stop=True)
                    nc.tensor.matmul(G.ps[:, 2 + 2 * (j % 2), 0:I], xqT[:, j * P:(j + 1) * P], wuT[:, 0:I],
                                     start=True, stop=True).then_inc(gu_made, 1)
                pe.wait_ge(own, FIRST + 2 * FP4_OPS * q + FP4_OPS)
                pe.wait_ge(added, q)

                def turn(j):
                    pe.wait_ge(h_copied, QUAD * q + max(j - 1, 0))
                    for c, (lo, rows) in enumerate(CH):
                        mm = nc.tensor.transpose(G.ps[0:rows, (5, 7)[j % 2], c * P:(c + 1) * P], hid[:, j, lo:lo + rows],
                                                 G.c["ident"])
                    mm.then_inc(h_turned, 1)

                turn(0)
                for j in range(QUAD):
                    if j + 1 < QUAD:
                        turn(j + 1)
                    pe.wait_ge(h_copied, QUAD * q + j + 1)
                    for c, (lo, rows) in enumerate(CH):
                        mm = nc.tensor.matmul(G.ps[:, 6, j * P:(j + 1) * P], hidT[0:rows, j % 2, c, :], wdT[0:rows, c, :],
                                              start=c == 0, stop=c == 2)
                    mm.then_inc(out_made, 1) if j == QUAD - 1 else mm.then_inc(own_pe, 1)

        @block.scalar
        def _(act):
            act.wait_ge(w_turned, 1)
            nc.scalar.copy(wgT[:, 0:I], G.ps[:, 0, 0:I])
            nc.scalar.copy(wuT[:, 0:I], G.ps[:, 1, 0:I])
            nc.scalar.copy(wdT[:, 0:2, :].rearrange("p c d -> p (c d)"), G.ps[:, 2, 0:2 * P])
            nc.scalar.copy(wdT[0:96, 2, :], G.ps[0:96, 2, 2 * P:3 * P]).then_inc(w_copied, 1)
            with act.Fori(0, NQ) as q:
                act.wait_ge(x_turned, q + 1)
                act.wait_ge(gu_made, QUAD * q)
                nc.scalar.copy(xqT[:], G.ps[:, 0, :]).then_inc(x_copied, 1)
                for j in range(QUAD):
                    act.wait_ge(gu_made, QUAD * q + j + 1)
                    act.wait_ge(h_made, QUAD * q + max(j - 1, 0))
                    nc.scalar.activation(gate[:, j % 2, :], G.ps[:, 1 + 2 * (j % 2), 0:I], ACT.Silu).then_inc(gated, 1)
                for j in range(QUAD):
                    act.wait_ge(h_turned, QUAD * q + j + 1)
                    if j < 2:
                        act.wait_ge(out_made, q)
                    else:
                        act.wait_ge(own_pe, (QUAD - 1) * q + j - 1)
                    bank = (5, 7)[j % 2]
                    nc.scalar.copy(hidT[:, j % 2, 0:2, :].rearrange("p c t -> p (c t)"), G.ps[:, bank, 0:2 * P])
                    nc.scalar.copy(hidT[0:96, j % 2, 2, :], G.ps[0:96, bank, 2 * P:3 * P]).then_inc(h_copied, 1)


def l3_attn(nc, G):
    w = G.w["l3_attn"]
    H, DH, CH = 8, 64, 4
    layernorm(nc, G, "l3_attn", "l3_attn")
    with Scope(nc, G, "l3_attn") as s:
        decay = s.sb("decay", [P, CH])
        rest = s.sb("rest", [P, CH])
        rest_bv = s.sb("rest_bv", [P, CH])
        keep = s.sb("keep", [P, CH, QUAD, P])
        q_sb = s.sb("q", [P, CH, QT])
        qk = s.sb("qk", [P, CH, QT])
        s_row = s.sb("s_row", [H, QT])
        top = s.sb("top", [P, QUAD])
        probs = s.sb("probs", [P, QUAD, H])
        probsT = s.sb("probsT", [H, QT])
        v_sb = s.sb("v", [P, 2, QT])
        fed = s.sb("fed", [P, 2, QT])
        state = s.sb("state", [P, 2, QT])
        aug = s.sb("aug", [P, 2, QT])
        o = s.sb("o", [P, CH, QT])
        (own, dec_set, q_made, q_set, qk_set, s_made, s_copied, s_turned, shifted, exped, p_set, p_turned, p_copied,
         v_made, v_set, fed_set, aug_set, prod_set, o_set, out_made, out_copied, keep_set) = (s.sem(n) for n in (
             "own", "dec_set", "q_made", "q_set", "qk_set", "s_made", "s_copied", "s_turned", "shifted", "exped", "p_set",
             "p_turned", "p_copied", "v_made", "v_set", "fed_set", "aug_set", "prod_set", "o_set", "out_made",
             "out_copied", "keep_set"))
        block = s.block()

        @block.tensor
        def _(pe):
            with pe.Fori(0, NQ) as q:
                tokens = G.xnT[:, bass.ds(q * QUAD, QUAD), :]
                for c in range(CH):
                    pe.wait_ge(qk_set, CH * q + max(c - 1, 0))
                    nc.tensor.matmul(G.ps[:, c % 2, :], w["wq"][:, c * P:(c + 1) * P], tokens, start=True, stop=True)
                    nc.tensor.matmul(G.ps[:, 2 + c % 2, :], w["wk"][:, c * P:(c + 1) * P], tokens, start=True, stop=True)\
                      .then_inc(q_made, 1)
                pe.wait_ge(qk_set, CH * (q + 1))
                pe.wait_ge(out_copied, q)
                for c in range(CH):
                    mm = nc.tensor.matmul(G.ps[0:H, 4, :], w["heads"][:, c * H:(c + 1) * H], qk[:, c, :], start=c == 0,
                                          stop=c == CH - 1)
                mm.then_inc(s_made, 1)
                pe.wait_ge(s_copied, q + 1)
                for j in range(QUAD):
                    mm = nc.tensor.matmul(G.ps[:, 5, j * H:(j + 1) * H], s_row[:, j * P:(j + 1) * P],
                                          G.c["ident"][0:H, 0:H], start=True, stop=True)
                mm.then_inc(s_turned, 1)
                pe.wait_ge(p_set, q + 1)
                for j in range(QUAD):
                    mm = nc.tensor.transpose(G.ps[0:H, 5, j * P:(j + 1) * P], probs[:, j, :], G.c["ident"])
                mm.then_inc(p_turned, 1)
                pe.wait_ge(p_copied, q + 1)
                for c in range(CH):
                    pe.wait_ge(fed_set, CH * q + c)
                    nc.tensor.matmul(G.ps[:, 6, :], w["wv"][:, c * P:(c + 1) * P], tokens, start=True, stop=True)
                    nc.tensor.matmul(G.ps[:, 7, :], G.c["sel_e"][:, c * P:(c + 1) * P], probsT[:], start=True, stop=True)\
                      .then_inc(v_made, 1)
                pe.wait_ge(o_set, CH * (q + 1))
                for j in range(QUAD):
                    for c in range(CH):
                        nc.tensor.matmul(G.ps[:, 4, j * P:(j + 1) * P], o[:, c, j * P:(j + 1) * P],
                                         w["wo"][:, c * D:(c + 1) * D], start=c == 0, stop=False)
                    mm = nc.tensor.matmul(G.ps[:, 4, j * P:(j + 1) * P], G.c["ones_row"], w["bo"], start=False, stop=True)
                mm.then_inc(out_made, 1)

        @block.scalar
        def _(act):
            nc.scalar.activation(decay[:], w["alpha"], ACT.Sigmoid).then_inc(dec_set, 1)
            act.wait_ge(keep_set, 1)
            with act.Fori(0, NQ) as q:
                act.wait_ge(prod_set, CH * q)
                for c in range(CH):
                    act.wait_ge(q_made, CH * q + c + 1)
                    nc.scalar.activation(q_sb[:, c, :], G.ps[:, c % 2, :], ACT.Identity, bias=w["bq"][:, c:c + 1])\
                      .then_inc(q_set, 1)
                act.wait_ge(s_made, q + 1)
                nc.scalar.copy(s_row[:], G.ps[0:H, 4, :]).then_inc(s_copied, 1)
                act.wait_ge(shifted, q + 1)
                nc.scalar.activation(probs[:], probs[:], ACT.Exp, scale=DH ** -0.5).then_inc(exped, 1)
                act.wait_ge(p_turned, q + 1)
                nc.scalar.copy(probsT[:], G.ps[0:H, 5, :]).then_inc(p_copied, 1)
                for c in range(CH):
                    act.wait_ge(v_made, CH * q + c + 1)
                    act.wait_ge(fed_set, CH * q + max(c - 1, 0))
                    nc.scalar.activation(v_sb[:, c % 2, :], G.ps[:, 6, :], ACT.Identity, bias=rest_bv[:, c:c + 1],
                                         scale=rest[:, c:c + 1]).then_inc(v_set, 1)
                    act.wait_ge(o_set, CH * q + max(c - 1, 0))
                    nc.scalar.activation(aug[:, c % 2, :], q_sb[:, c, :], ACT.Sigmoid, scale=w["aug"][:, c:c + 1])\
                      .then_inc(aug_set, 1)
                act.wait_ge(out_made, q + 1)
                nc.scalar.copy(G.xn[:, bass.ds(q * QUAD, QUAD), :], heads4(G.ps[:, 4, :])).then_inc(out_copied, 1)

        @block.vector
        def _(dve):
            dve.wait_ge(dec_set, 1)
            link = Link(dve, own)
            link.note(nc.vector.memset(keep[:], 1.0))
            link(nc.vector.tensor_scalar(rest[:], decay[:], -1.0, 1.0, ALU.mult, ALU.add))
            for c in range(CH):
                link.note(nc.vector.tensor_scalar(keep[:, c, :, :], keep[:, c, :, :], decay[:, c:c + 1], None, ALU.mult))
            link.catch()
            link.note(nc.vector.memset(keep[:, :, :, 0:1], 0.0))
            nc.vector.tensor_tensor(rest_bv[:], rest[:], w["bv"], ALU.mult).then_inc(keep_set, 1)
            link.catch()
            base, per = link.n, 3 + CH
            with dve.Fori(0, NQ) as q:
                link = Link(dve, own, base + per * q)
                for c in range(CH):
                    dve.wait_ge(q_set, CH * q + c + 1)
                    nc.vector.scalar_tensor_tensor(qk[:, c, :], G.ps[:, 2 + c % 2, :], w["bk"][:, c:c + 1], q_sb[:, c, :],
                                                   ALU.add, ALU.mult).then_inc(qk_set, 1)
                dve.wait_ge(s_turned, q + 1)
                scores = G.ps[:, 5, 0:QUAD * H].rearrange("p (b h) -> p b h", b=QUAD)
                link(nc.vector.tensor_reduce(top[:], scores, AX.X, ALU.max))
                nc.vector.tensor_tensor(probs[:], scores, along(top[:], [P, QUAD, H]), ALU.subtract).then_inc(shifted, 1)
                dve.wait_ge(exped, q + 1)
                link(nc.vector.tensor_reduce(top[:], probs[:], AX.X, ALU.add))
                link(nc.vector.reciprocal(top[:], top[:]))
                nc.vector.tensor_tensor(probs[:], probs[:], along(top[:], [P, QUAD, H]), ALU.mult).then_inc(p_set, 1)
                for c in range(CH):
                    slot = c % 2
                    dve.wait_ge(v_set, CH * q + c + 1)
                    nc.vector.tensor_tensor(fed[:, slot, :], v_sb[:, slot, :], G.ps[:, 7, :], ALU.mult).then_inc(fed_set, 1)
                    dve.wait_ge(fed_set, CH * q + c + 1)
                    link(nc.vector.tensor_tensor_scan(state[:, slot, :], keep[:, c, :, :].rearrange("p b t -> p (b t)"),
                                                      fed[:, slot, :], 0.0, ALU.mult, ALU.add))
                    nc.vector.tensor_tensor(state[:, slot, :], state[:, slot, :], q_sb[:, c, :], ALU.mult)\
                      .then_inc(prod_set, 1)
                    dve.wait_ge(prod_set, CH * q + c + 1)
                    dve.wait_ge(aug_set, CH * q + c + 1)
                    dve.wait_ge(out_made, q)
                    nc.vector.tensor_tensor(o[:, c, :], state[:, slot, :], aug[:, slot, :], ALU.add).then_inc(o_set, 1)

    with Scope(nc, G, "l3_attn_ln") as s:
        mean, rs, rstd, stats_of, rstd_of = row_stats(nc, s, lambda b: G.xn[:, b, :], 1e-6)
        own = s.sem("own")
        block = s.block()

        @block.gpsimd
        def _(pool):
            for half in range(2):
                rstd_of(pool, half)

        @block.vector
        def _(dve):
            stats_of(dve, 0)
            stats_of(dve, 1)
            dve.wait_ge(rstd, 2)
            with dve.Fori(0, NB) as b:
                nc.vector.tensor_scalar(G.xn[:, b, :], G.xn[:, b, :], mean[:, bass.ds(b, 1)], rs[:, bass.ds(b, 1)],
                                        ALU.subtract, ALU.mult).then_inc(own, 1)
            dve.wait_ge(own, NB)
            link = Link(dve, own, NB)
            link(nc.vector.tensor_tensor(G.xn[:], G.xn[:], w["ln_scale"].unsqueeze(1).broadcast_to([P, NB, D]), ALU.mult))
            link(nc.vector.tensor_tensor(G.xn[:], G.xn[:], w["ln_bias"].unsqueeze(1).broadcast_to([P, NB, D]), ALU.add))
            link(nc.vector.tensor_tensor(G.x[:], G.x[:], G.xn[:], ALU.add))


def l3_rwkv(nc, G):
    w = G.w["l3_rwkv"]
    W = P + 2
    layernorm(nc, G, "l3_rwkv", "l3_rwkv")
    with Scope(nc, G, "l3_rwkv") as s:
        ew = s.sb("ew", [P, 1])
        keep = s.sb("keep", [P, QUAD, W])
        ek = s.sb("ek", [P, 2, QUAD, W])
        ekv = s.sb("ekv", [P, 2, QUAD, W])
        cur = s.sb("cur", [P, 2, QUAD, P])
        cur_v = s.sb("cur_v", [P, 2, QUAD, P])
        r = s.sb("r", [P, NB, P])
        scans = [s.sb(f"scan{n}", [P, QUAD, W]) for n in range(4)]
        num = s.sb("num", [P, QUAD, P])
        den = s.sb("den", [P, QUAD, P])
        wkv = s.sb("wkv", [P, 2, QUAD, P])
        (own, zeroed, ew_set, keep_set, r_set, cur_set, kv_set, scanned, wkv_set, turned, added) = (s.sem(n) for n in (
            "own", "zeroed", "ew_set", "keep_set", "r_set", "cur_set", "kv_set", "scanned", "wkv_set", "turned", "added"))
        block = s.block()

        def pairs(eng, body):
            with eng.Fori(0, NQ // 2) as i:
                for k in range(2):
                    body(2 * i + k, k, i)

        @block.scalar
        def _(act):
            nc.scalar.activation(r[:], G.xnT[:], ACT.Sigmoid).then_inc(r_set, 1)
            nc.scalar.activation(ew[:], w["w"], ACT.Exp).then_inc(ew_set, 1)
            act.wait_ge(zeroed, 1)

            def body(q, slot, i):
                keys = G.ctxT[:, bass.ds(q * QUAD, QUAD), :]
                act.wait_ge(wkv_set, 2 * i)
                nc.scalar.activation(ek[:, slot, :, 1:1 + P], keys, ACT.Exp)
                nc.scalar.activation(cur[:, slot, :, :], keys, ACT.Exp, bias=w["u"]).then_inc(cur_set, 1)

            pairs(act, body)

        @block.gpsimd
        def _(pool):
            nc.gpsimd.memset(ek[:], 0.0)
            nc.gpsimd.memset(ekv[:], 0.0).then_inc(zeroed, 1)
            pool.wait_ge(zeroed, 1)

            def body(q, slot, i):
                values = G.ctxT[:, bass.ds(q * QUAD, QUAD), :]
                pool.wait_ge(cur_set, q + 1)
                nc.gpsimd.tensor_tensor(ekv[:, slot, :, 1:1 + P], ek[:, slot, :, 1:1 + P], values, ALU.mult)
                nc.gpsimd.tensor_tensor(cur_v[:, slot, :, :], cur[:, slot, :, :], values, ALU.mult).then_inc(kv_set, 1)

            pairs(pool, body)

        @block.vector
        def _(dve):
            link = Link(dve, own)
            link(nc.vector.memset(keep[:], 0.0))
            link(nc.vector.memset(keep[:, :, 1:1 + P], 1.0))
            dve.wait_ge(ew_set, 1)
            flat = lambda a: a.rearrange("p b t -> p (b t)")
            link(nc.vector.tensor_scalar(flat(keep[:]), flat(keep[:]), ew[:, 0:1], None, ALU.mult))
            dve.wait_ge(r_set, 1)
            PER = 7 + 3

            def body(q, slot, i):
                link = Link(dve, own, 3 + PER * q)
                dve.wait_ge(kv_set, q + 1)
                a_f, b_f, a_b, b_b = scans
                for out, data, step in ((a_f, ekv, 1), (b_f, ek, 1), (a_b, ekv, -1), (b_b, ek, -1)):
                    link.note(nc.vector.tensor_tensor_scan(flat(out[:])[:, ::step], flat(keep[:])[:, ::step],
                                                           flat(data[:, slot, :, :])[:, ::step], 0.0, ALU.mult, ALU.add))
                link.catch()
                link.note(nc.vector.tensor_tensor(num[:], a_f[:, :, 0:P], a_b[:, :, 2:2 + P], ALU.add))
                link(nc.vector.tensor_tensor(den[:], b_f[:, :, 0:P], b_b[:, :, 2:2 + P], ALU.add))
                link.note(nc.vector.tensor_tensor(num[:], num[:], cur_v[:, slot, :, :], ALU.add))
                link(nc.vector.tensor_tensor(den[:], den[:], cur[:, slot, :, :], ALU.add))
                link(nc.vector.reciprocal(den[:], den[:]))
                dve.wait_ge(turned, 2 * i)
                link(nc.vector.tensor_tensor(num[:], num[:], den[:], ALU.mult))
                nc.vector.tensor_tensor(wkv[:, slot, :, :], num[:], r[:, bass.ds(q * QUAD, QUAD), :], ALU.mult)\
                  .then_inc(wkv_set, 1)
                dve.wait_ge(turned, q + 1)
                x = G.x[:, bass.ds(q * QUAD, QUAD), :]
                nc.vector.tensor_tensor(x, x, heads4(G.ps[:, slot, :]), ALU.add).then_inc(added, 1)

            pairs(dve, body)

        @block.tensor
        def _(pe):
            def body(q, slot, i):
                pe.wait_ge(wkv_set, q + 1)
                pe.wait_ge(added, 2 * i)
                for j in range(QUAD):
                    mm = nc.tensor.transpose(G.ps[:, slot, j * P:(j + 1) * P], wkv[:, slot, j, :], G.c["ident"])
                mm.then_inc(turned, 1)

            pairs(pe, body)


def l3_moe(nc, G):
    w = G.w["l3_moe"]
    E, CH = 14, 2
    layernorm(nc, G, "l3_moe", "l3_moe")
    with Scope(nc, G, "l3_moe") as s:
        logits = s.sb("logits", [P, NB, E])
        probs = s.sb("probs", [P, NB, E])
        top8 = s.sb("top8", [P, NB, 8])
        work = s.sb("work", [P, 4, NB, E])
        gates = s.sb("gates", [P, NB, E])
        total = s.sb("total", [P, NB])
        gatesT = s.sb("gatesT", [E, NB, P])
        hidden = s.sb("hidden", [P, 2, CH, QT])
        (scored, own, own_top, shifted, exped, gates_set, turned, gatesT_set, biased, h_made, gelued, y_made, summed,
         clipped, added) = (s.sem(n) for n in (
             "scored", "own", "own_top", "shifted", "exped", "gates_set", "turned", "gatesT_set", "biased", "h_made",
             "gelued", "y_made", "summed", "clipped", "added"))
        block = s.block()

        @block.tensor
        def _(pe):
            for b in range(NB):
                mm = nc.tensor.matmul(G.ps[:, 0, b * E:(b + 1) * E], G.xnT[:, b, :], w["gate"], start=True, stop=True)
            mm.then_inc(scored, 1)
            pe.wait_ge(gates_set, 1)
            for b in range(NB):
                mm = nc.tensor.transpose(G.ps[0:E, 4 + b // 4, (b % 4) * P:(b % 4 + 1) * P], gates[:, b, :], G.c["ident"])
            mm.then_inc(turned, 1)
            pe.wait_ge(gatesT_set, 1)
            for b in range(NB):
                mm = nc.tensor.matmul(G.ps[:, 4 + b // 4, (b % 4) * P:(b % 4 + 1) * P], gatesT[:, b, :], w["b2"],
                                      start=True, stop=True)
            mm.then_inc(turned, 1)
            pe.wait_ge(biased, 1)
            with pe.Fori(0, NQ) as q:
                tokens = G.xnT[:, bass.ds(q * QUAD, QUAD), :]

                def first(e):
                    pe.wait_ge(gelued, E * q + max(e - 1, 0))
                    for c in range(CH):
                        mm = nc.tensor.matmul(G.ps[:, 2 * (e % 2) + c, :], w["w1"][:, (e * CH + c) * P:(e * CH + c + 1) * P],
                                              tokens, start=True, stop=True)
                    mm.then_inc(h_made, 1)

                def second(e):
                    pe.wait_ge(gelued, E * q + e + 1)
                    pe.wait_ge(summed, QUAD * (E * q + max(e - 1, 0)))
                    for j in range(QUAD):
                        for c in range(CH):
                            mm = nc.tensor.matmul(G.ps[:, 4 + e % 2, j * P:(j + 1) * P],
                                                  hidden[:, e % 2, c, j * P:(j + 1) * P],
                                                  w["w2"][:, (e * CH + c) * D:(e * CH + c + 1) * D], start=c == 0,
                                                  stop=c == CH - 1)
                    mm.then_inc(y_made, 1)

                first(0)
                for e in range(E):
                    if e + 1 < E:
                        first(e + 1)
                    second(e)

        @block.scalar
        def _(act):
            act.wait_ge(shifted, 1)
            nc.scalar.activation(probs[:], logits[:], ACT.Exp).then_inc(exped, 1)
            act.wait_ge(turned, 1)
            nc.scalar.copy(gatesT[:].rearrange("p b t -> p (b t)"),
                           G.ps[0:E, 4:8, :].rearrange("p b t -> p (b t)")).then_inc(gatesT_set, 1)
            with act.Fori(0, NQ) as q:
                for e in range(E):
                    act.wait_ge(h_made, E * q + e + 1)
                    act.wait_ge(y_made, E * q + max(e - 1, 0))
                    for c in range(CH):
                        ins = nc.scalar.activation(hidden[:, e % 2, c, :], G.ps[:, 2 * (e % 2) + c, :], ACT.Gelu,
                                                   bias=w["b1"][:, e * CH + c:e * CH + c + 1])
                    ins.then_inc(gelued, 1)

        @block.vector
        def _(dve):
            dve.wait_ge(scored, 1)
            link = Link(dve, own)
            by_row = lambda a: along(a, [P, NB, E])
            ps_logits = G.ps[:, 0, 0:NB * E].rearrange("p (b e) -> p b e", e=E)
            link(nc.vector.tensor_reduce(total[:], ps_logits, AX.X, ALU.max))
            nc.vector.tensor_tensor(logits[:], ps_logits, by_row(total[:]), ALU.subtract).then_inc(shifted, 1)
            dve.wait_ge(exped, 1)
            link(nc.vector.tensor_reduce(total[:], probs[:], AX.X, ALU.add))
            link(nc.vector.reciprocal(total[:], total[:]))
            link(nc.vector.tensor_tensor(probs[:], probs[:], by_row(total[:]), ALU.mult))
            best = top_two(nc, dve, own_top, G, probs[:], top8[:], work[:], gates[:], E)
            best(nc.vector.tensor_tensor(gates[:], gates[:], probs[:], ALU.mult))
            best(nc.vector.tensor_tensor(total[:], top8[:, :, 0], top8[:, :, 1], ALU.add))
            best(nc.vector.tensor_scalar(total[:], total[:], 1e-10, None, ALU.max))
            best(nc.vector.reciprocal(total[:], total[:]))
            nc.vector.tensor_tensor(gates[:], gates[:], by_row(total[:]), ALU.mult).then_inc(gates_set, 1)
            dve.wait_ge(turned, 2)
            nc.vector.tensor_tensor(G.xn[:].rearrange("p b d -> p (b d)"), G.xn[:].rearrange("p b d -> p (b d)"),
                                    G.ps[:, 4:8, :].rearrange("p b d -> p (b d)"), ALU.add).then_inc(biased, 1)
            dve.wait_ge(biased, 1)
            dve.wait_ge(gates_set, 1)
            with dve.Fori(0, NQ) as q:
                for e in range(E):
                    dve.wait_ge(y_made, E * q + e + 1)
                    dve.wait_ge(summed, QUAD * (E * q + e))
                    for j in range(QUAD):
                        b = q * QUAD + j
                        nc.vector.scalar_tensor_tensor(G.xn[:, b, :], G.ps[:, 4 + e % 2, j * P:(j + 1) * P],
                                                       gates[:, b, e:e + 1], G.xn[:, b, :], ALU.mult, ALU.add)\
                          .then_inc(summed, 1)
                quad = bass.ds(q * QUAD, QUAD)
                dve.wait_ge(summed, QUAD * E * (q + 1))
                nc.vector.tensor_scalar(G.xn[:, quad, :], G.xn[:, quad, :], 100.0, -100.0, ALU.min, ALU.max)\
                  .then_inc(clipped, 1)
                dve.wait_ge(clipped, q + 1)
                nc.vector.tensor_tensor(G.x[:, quad, :], G.x[:, quad, :], G.xn[:, quad, :], ALU.add).then_inc(added, 1)


def load(nc, G, aps):
    @G.first.sync
    def _(sp):
        half = NB // 2
        for n in range(2):
            sp.dma_start(G.x[:, n * half:(n + 1) * half, :], aps["x"][:, n * half:(n + 1) * half, :])\
              .then_inc(G.loaded[f"x{n}"], 16)
        for group in LAYOUT:
            if group == "l3_moe":
                continue
            sp.dma_start(G.pack[group], aps[group]).then_inc(G.loaded[group], 16)
            if group == "l0_attn":
                sp.dma_start(G.ctxT[:], aps["ctxT"]).then_inc(G.loaded["ctxT"], 16)
                sp.dma_start(G.ctx1[:], aps["ctx1"]).then_inc(G.loaded["ctx1"], 16)


def small_constants(nc, G, dve):
    dve.wait_ge(G.loaded["const"], 16)
    nc.vector.memset(G.ones[:], 1.0)
    nc.vector.tensor_copy(G.ident_bf[:], G.c["ident"])
    nc.vector.tensor_copy(G.rows3_bf[:], G.c["rows3"])
    nc.vector.tensor_copy(G.mask_qk_bf[:], G.c["mask_qk"])
    nc.vector.tensor_copy(G.mask_kq_bf[:], G.c["mask_kq"])


def store(nc, G, out):
    with Scope(nc, G, "store") as s:
        stored = s.sem("stored")
        block = s.block()

        @block.sync
        def _(sp):
            sp.dma_start(out, G.x[:]).then_inc(stored, 16)
            sp.wait_ge(stored, 16)


SUBLAYERS = [l0_attn, l0_mlstm, l0_moe, l1_attn, l1_xattn, l1_ffn, l2_mamba, l2_xattn, l2_ffn, l3_attn, l3_rwkv, l3_moe]


class State:

    def __init__(self):
        self.pack, self.w, self.loaded, self.spent, self.cleared, self.started = {}, {}, {}, [], [], False


def program(nc, aps, out, sublayers=None):
    stack = ExitStack()
    with stack:
        G = State()

        def sb(name, shape, dt=F32):
            return stack.enter_context(nc.sbuf_tensor(name, shape, dt))

        G.x = sb("x", [P, NB, D])
        G.xn = sb("xn", [P, NB, D])
        G.xnT = sb("xnT", [P, NB, P])
        G.ctxT = sb("ctxT", [P, NB, P])
        G.ctx1 = sb("ctx1", [P, NB, 8 * 17])
        G.aps = aps
        G.ones = sb("ones", [P, 512])
        G.ident_bf = sb("ident_bf", [P, P], BF16)
        G.rows3_bf = sb("rows3_bf", [96, 32], BF16)
        G.mask_qk_bf = sb("mask_qk_bf", [P, P], BF16)
        G.mask_kq_bf = sb("mask_kq_bf", [P, P], BF16)
        for name in ("x0", "x1", "ctxT", "ctx1", *LAYOUT):
            G.loaded[name] = stack.enter_context(nc.semaphore(f"loaded_{name}"))
        shared = sb("w_early", [P, max(sum(spans(g)[1] for g in EARLY), spans("l3_moe")[1])])
        at = 0
        for group in LAYOUT:
            cols, total = spans(group)
            if group in EARLY:
                G.pack[group] = shared[:, at:at + total]
                at += total
            elif group == "l3_moe":
                G.pack[group] = shared[:, 0:total]
            else:
                G.pack[group] = sb(f"w_{group}", [P, total])[:]
            G.w[group] = {n: G.pack[group][0:r, a:b] for n, (r, a, b) in cols.items()}
        G.c = G.w["const"]
        G.c["ones_row"] = G.ones[0:1, 0:P]
        G.ps = stack.enter_context(nc.psum_tensor("ps", [P, 8, 512], F32))
        with nc.Block() as first:
            G.first = first
            load(nc, G, aps)
        for sublayer in sublayers or SUBLAYERS:
            sublayer(nc, G)
        store(nc, G, out)


def constants():
    t = np.arange(P)
    n_values = 256 - 16 + 1
    values = 1.0 - np.power(np.linspace(0.0, 1.0, n_values, dtype=np.float32), np.float32(1.0 / np.e))
    values = np.concatenate([np.ones(15, np.float32), values.astype(np.float32)])
    back = t[:, None] - t[None, :]
    decay = np.where(back >= 0, values[np.clip(back, 0, P - 1)], 0.0)
    later = np.where(back >= 0, 0.0, NEG)
    heads = np.repeat(np.eye(16), 8, axis=0)
    heads16 = np.repeat(np.eye(8), 16, axis=0) / 4.0
    sel_e = np.repeat(np.eye(8), 64, axis=1)
    pairs = np.zeros((P, 8))
    pairs[2 + 2 * np.arange(8), np.arange(8)] = 1.0
    return dict(ident=np.eye(P), mask_qk=later, mask_kq=later.T, decay=decay.T, heads=heads, heads16=heads16, sel_e=sel_e,
                pairs=pairs, rows3=np.tile(np.eye(32), (3, 1)))


def by_rows(w, rows=P):
    n = w.shape[0] // rows
    return w.reshape(n, rows, -1).transpose(1, 0, 2).reshape(rows, -1)


def by_feature(v, rows=P):
    return v.reshape(-1, rows).T


def heads_of_64(w):
    return w.reshape(-1, 2, 2, 4, 64).transpose(0, 1, 3, 2, 4).reshape(-1, 1024)


def bc_first(w):
    return np.concatenate([w[:, 64:], np.zeros_like(w[:, 64:]), w[:, :64]], axis=1)


def laid_out(a):
    wa = a["L0_attn_W_attn"]
    L = {"const": constants()}
    L["l0_attn"] = dict(wq=wa[:, :128], wk=wa[:, 128:256], wv=wa[:, 256:], wo=a["L0_attn_W_proj"])
    gates = a["L0_xattn_ifgate_w"]
    L["l0_mlstm"] = dict(wg=by_rows(gates.T), bias=np.tile(a["L0_xattn_ifgate_b"].reshape(2, 8), (1, NB)).T,
                         gain=np.broadcast_to(a["L0_xattn_outnorm_w"], (P, D)))
    L["l0_moe"] = dict(wg=a["L0_ffn_w_gate"], wd=a["L0_ffn_Wd"].transpose(1, 0, 2).reshape(D, 512),
                       bd=by_feature(a["L0_ffn_bd"]), wu=by_rows(a["L0_ffn_Wu"].reshape(512, D)), bu=a["L0_ffn_bu"])
    L["l1_attn"] = dict(rot=a["L1_attn_rotation_params"].reshape(D, 1), ent=a["L1_attn_entangle_params"].reshape(D, 1))
    wkv = a["L1_xattn_Wkv"]
    L["l1_xattn"] = dict(ln_g=by_feature(a["L1_xattn_ln_g"]), ln_b=by_feature(a["L1_xattn_ln_b"]),
                         cln_g=by_feature(a["L1_xattn_cln_g"]), cln_b=by_feature(a["L1_xattn_cln_b"]),
                         wq=heads_of_64(a["L1_xattn_Wq"]), wkk=np.tile(wkv[:, :64], (1, 2)), wv=wkv[:, 64:],
                         wo=by_rows(a["L1_xattn_Wo"]), wff1=a["L1_xattn_Wff1"], wff2=by_rows(a["L1_xattn_Wff2"]))
    L["l1_ffn"] = dict(w1=a["L1_ffn_W1"].T, b1=by_feature(a["L1_ffn_b1"]), w2=by_rows(a["L1_ffn_W2"].T),
                       b2=a["L1_ffn_b2"][None, :], scale=np.broadcast_to(a["L1_ffn_scale"], (P, 1)))
    L["l2_mamba"] = dict(w_in=a["L2_attn_W_in"], conv_w=by_rows(a["L2_attn_conv_w"].reshape(2 * P, 4)),
                         conv_b=by_feature(a["L2_attn_conv_b"]), w_x=by_rows(bc_first(a["L2_attn_W_x"])),
                         w_dt=np.concatenate([np.zeros_like(a["L2_attn_W_dt"]), a["L2_attn_W_dt"]]),
                         b_dt=by_feature(a["L2_attn_b_dt"]), a_log=by_rows(a["L2_attn_A_log"]),
                         d_skip=by_feature(a["L2_attn_D_param"]), w_out=by_rows(a["L2_attn_W_out"]))
    L["l2_xattn"] = dict(wq=heads_of_64(a["L2_xattn_W_q"]), wk=heads_of_64(a["L2_xattn_W_k"]), wv=a["L2_xattn_W_v"],
                         wo=by_rows(a["L2_xattn_W_out"]), b_out=a["L2_xattn_b_out"][None, :], bias=a["fside_SxS2_0"])
    rows352 = lambda m: by_rows(np.concatenate([m, np.zeros((384 - 352, D), m.dtype)]))
    L["l2_ffn"] = dict(wg=rows352(a["L2_ffn_w_gate"]), wu=rows352(a["L2_ffn_w_up"]), wd=a["L2_ffn_w_down"])
    heads = np.zeros((P, 4, 8))
    for c in range(4):
        heads[np.arange(P), c, 2 * c + np.arange(P) // 64] = 1.0
    b = lambda n: by_feature(a["L3_attn_" + n].reshape(-1))
    L["l3_attn"] = dict(wq=a["L3_attn_Wq"], wk=a["L3_attn_Wk"], wv=a["L3_attn_Wv"], bq=b("bq"), bk=b("bk"), bv=b("bv"),
                        wo=by_rows(a["L3_attn_Wo"]), bo=a["L3_attn_bo"][None, :], alpha=b("alpha"), aug=b("aug_param"),
                        ln_scale=np.broadcast_to(a["L3_attn_ln_scale"], (P, D)),
                        ln_bias=np.broadcast_to(a["L3_attn_ln_bias"], (P, D)), heads=heads.reshape(P, 32))
    L["l3_rwkv"] = dict(w=a["L3_xattn_w"].reshape(P, 1), u=a["L3_xattn_u"].reshape(P, 1))
    L["l3_moe"] = dict(gate=a["L3_ffn_gate_w"].T, w1=a["L3_ffn_w1"].transpose(1, 0, 2).reshape(D, -1),
                       b1=by_feature(a["L3_ffn_b1"]), w2=by_rows(a["L3_ffn_w2"].reshape(-1, D)), b2=a["L3_ffn_b2"])
    return L


def packed(group, arrays):
    cols, total = spans(group)
    out = np.zeros((P, total), np.float32)
    for name, (rows, lo, hi) in cols.items():
        out[0:rows, lo:hi] = arrays[name]
    return out


def host_arrays(a):
    a = {k: np.asarray(v) for k, v in a.items()}
    arrays = {g: packed(g, v) for g, v in laid_out(a).items()}
    ctx = a["ctx_1024"]
    arrays["x"] = np.ascontiguousarray(a["x"].transpose(1, 0, 2))
    arrays["ctxT"] = np.ascontiguousarray(ctx.transpose(2, 0, 1))
    ctx1 = np.ones((P, NB, 8, 17), np.float32)
    ctx1[..., :16] = ctx.reshape(NB, P, 8, 16).transpose(1, 0, 2, 3)
    arrays["ctx1"] = ctx1.reshape(P, NB, 8 * 17)
    return arrays


def kernel(**inputs):
    from concourse import bacc
    from concourse.bass_utils import run_bass_kernel_spmd

    nc = bacc.Bacc("TRN2", target_bir_lowering=False, num_devices=1)
    arrays = host_arrays(inputs)
    aps = {n: nc.dram_tensor(f"in_{n}", a.shape, F32, kind="ExternalInput").ap() for n, a in arrays.items()}
    out = nc.dram_tensor("out_x", (P, NB, D), F32, kind="ExternalOutput").ap()
    program(nc, aps, out)
    r = run_bass_kernel_spmd(nc, [{f"in_{n}": a for n, a in arrays.items()}], core_ids=[0])
    return np.ascontiguousarray(r.results[0]["out_x"].transpose(1, 0, 2))
```
